# Optimizing a Trainium2 kernel written in Bass

```python
import numpy as np
import jax
import jax.numpy as jnp

def _softmax(x, axis=-1):
    return jax.nn.softmax(x, axis=axis)

def _gelu(x):
    return jax.nn.gelu(x, approximate=True)

def _silu(x):
    return jax.nn.silu(x)

def _sigmoid(x):
    return jax.nn.sigmoid(x)

def _layernorm(x, axis=-1, eps=1e-05):
    m = jnp.mean(x, axis=axis, keepdims=True)
    v = jnp.var(x, axis=axis, keepdims=True)
    return (x - m) / jnp.sqrt(v + eps)

def _scatter_add(tgt, idx, src, axis=0):
    return tgt.at[idx].add(src)

def _segment_sum(src, seg, n):
    return jax.ops.segment_sum(src, seg, n)
kernel_name = 'mk_macaron_d1_jaxref_r8_70bdfe'

def setup_inputs(seed: int=0):
    np.random.seed(seed)
    _w = jnp.asarray

    def _L0_attn_setup():
        import jax, jax.numpy as jnp
        import numpy as np
        import math
        D_MODEL = 128
        N_HEADS = 16
        D_K = D_MODEL // N_HEADS
        D_FF = 512
        ROPE_THETA = 10000.0
        EPS = 1e-05

        def _rms_norm(x, w):
            rms = jnp.sqrt(EPS + jnp.mean(x * x, axis=-1, keepdims=True))
            return x / rms * w

        def _rope_tables(seq_len):
            pos = jnp.arange(seq_len, dtype=jnp.float32)
            k = jnp.arange(D_K) // 2
            angles = pos[:, None] / jnp.power(ROPE_THETA, 2.0 * k.astype(jnp.float32) / D_K)
            cos = jnp.cos(angles)
            sin = jnp.sin(angles)
            idx = jnp.arange(D_K)
            even = idx % 2 == 0
            sin = sin * jnp.where(even, -1.0, 1.0)
            pair_swaps = idx + jnp.where(even, 1, -1)
            return (cos, sin, pair_swaps)

        def _apply_rope(t, cos, sin, pair_swaps):
            return t * cos + t[..., pair_swaps] * sin
        key = jax.random.key(seed)
        ks = jax.random.split(key, 10)
        B, S = (4, 256)
        s = 0.02
        return {'x': jax.random.normal(ks[0], (B, S, D_MODEL), dtype=jnp.float32), 'wq': jax.random.normal(ks[1], (D_MODEL, D_MODEL), dtype=jnp.float32) * s, 'wk': jax.random.normal(ks[2], (D_MODEL, D_MODEL), dtype=jnp.float32) * s, 'wv': jax.random.normal(ks[3], (D_MODEL, D_MODEL), dtype=jnp.float32) * s, 'wo': jax.random.normal(ks[4], (D_MODEL, D_MODEL), dtype=jnp.float32) * s, 'norm1_w': jnp.ones((D_MODEL,), dtype=jnp.float32), 'norm2_w': jnp.ones((D_MODEL,), dtype=jnp.float32), 'w1': jax.random.normal(ks[5], (D_FF, D_MODEL), dtype=jnp.float32) * s, 'w2': jax.random.normal(ks[6], (D_MODEL, D_FF), dtype=jnp.float32) * s, 'w3': jax.random.normal(ks[7], (D_FF, D_MODEL), dtype=jnp.float32) * s}
    _L0_attn_in = _L0_attn_setup()

    def _L0_ffn_setup():
        import jax, jax.numpy as jnp
        import numpy as np
        D_IN, D_HID = (128, 512)

        def _ternary(key, shape):
            return jax.random.randint(key, shape, -1, 2).astype(jnp.float32)

        def _tlin(x, w, s):
            return jnp.einsum('bsi,oi->bso', x, w) * s
        key = jax.random.key(seed)
        ks = jax.random.split(key, 12)
        inv = lambda fan: 1.0 / np.sqrt(fan).astype(np.float32)
        return {'x': jax.random.normal(ks[0], (4, 256, D_IN), dtype=jnp.float32), 'w1_w': _ternary(ks[1], (D_HID, D_IN)), 'w1_s': jax.random.uniform(ks[2], (D_HID,), dtype=jnp.float32) * inv(D_IN), 'w2_w': _ternary(ks[3], (D_HID, D_IN)), 'w2_s': jax.random.uniform(ks[4], (D_HID,), dtype=jnp.float32) * inv(D_IN), 'h1_w': _ternary(ks[5], (D_HID, D_HID)), 'h1_s': jax.random.uniform(ks[6], (D_HID,), dtype=jnp.float32) * inv(D_HID), 'h2_w': _ternary(ks[7], (D_HID, D_HID)), 'h2_s': jax.random.uniform(ks[8], (D_HID,), dtype=jnp.float32) * inv(D_HID), 'w3_w': _ternary(ks[9], (D_IN, D_HID)), 'w3_s': jax.random.uniform(ks[10], (D_IN,), dtype=jnp.float32) * inv(D_HID)}
    _L0_ffn_in = _L0_ffn_setup()
    _d = {'L0_attn_x': _L0_attn_in['x'], 'L0_attn_wq': _L0_attn_in['wq'], 'L0_attn_wk': _L0_attn_in['wk'], 'L0_attn_wv': _L0_attn_in['wv'], 'L0_attn_wo': _L0_attn_in['wo'], 'L0_attn_norm1_w': _L0_attn_in['norm1_w'], 'L0_attn_norm2_w': _L0_attn_in['norm2_w'], 'L0_attn_w1': _L0_attn_in['w1'], 'L0_attn_w2': _L0_attn_in['w2'], 'L0_attn_w3': _L0_attn_in['w3'], 'L0_ffn_w1_w': _L0_ffn_in['w1_w'], 'L0_ffn_w1_s': _L0_ffn_in['w1_s'], 'L0_ffn_w2_w': _L0_ffn_in['w2_w'], 'L0_ffn_w2_s': _L0_ffn_in['w2_s'], 'L0_ffn_h1_w': _L0_ffn_in['h1_w'], 'L0_ffn_h1_s': _L0_ffn_in['h1_s'], 'L0_ffn_h2_w': _L0_ffn_in['h2_w'], 'L0_ffn_h2_s': _L0_ffn_in['h2_s'], 'L0_ffn_w3_w': _L0_ffn_in['w3_w'], 'L0_ffn_w3_s': _L0_ffn_in['w3_s']}
    _x0 = _d['L0_attn_x']
    _d['L0_attn_x'] = jax.random.normal(jax.random.fold_in(jax.random.key(seed), 1), (8, 512, 128), dtype=_x0.dtype)
    del _x0
    return _d

def reference(L0_attn_x, L0_attn_wq, L0_attn_wk, L0_attn_wv, L0_attn_wo, L0_attn_norm1_w, L0_attn_norm2_w, L0_attn_w1, L0_attn_w2, L0_attn_w3, L0_ffn_w1_w, L0_ffn_w1_s, L0_ffn_w2_w, L0_ffn_w2_s, L0_ffn_h1_w, L0_ffn_h1_s, L0_ffn_h2_w, L0_ffn_h2_s, L0_ffn_w3_w, L0_ffn_w3_s):

    def _L0_attn_ref(x, wq, wk, wv, wo, norm1_w, norm2_w, w1, w2, w3):
        import jax, jax.numpy as jnp
        import numpy as np
        import math
        D_MODEL = 128
        N_HEADS = 16
        D_K = D_MODEL // N_HEADS
        D_FF = 512
        ROPE_THETA = 10000.0
        EPS = 1e-05

        def _rms_norm(x, w):
            rms = jnp.sqrt(EPS + jnp.mean(x * x, axis=-1, keepdims=True))
            return x / rms * w

        def _rope_tables(seq_len):
            pos = jnp.arange(seq_len, dtype=jnp.float32)
            k = jnp.arange(D_K) // 2
            angles = pos[:, None] / jnp.power(ROPE_THETA, 2.0 * k.astype(jnp.float32) / D_K)
            cos = jnp.cos(angles)
            sin = jnp.sin(angles)
            idx = jnp.arange(D_K)
            even = idx % 2 == 0
            sin = sin * jnp.where(even, -1.0, 1.0)
            pair_swaps = idx + jnp.where(even, 1, -1)
            return (cos, sin, pair_swaps)

        def _apply_rope(t, cos, sin, pair_swaps):
            return t * cos + t[..., pair_swaps] * sin
        B, S, _ = x.shape
        h = _rms_norm(x, norm1_w)
        q = h @ wq.T
        k = h @ wk.T
        v = h @ wv.T

        def split_heads(t):
            return t.reshape(B, S, N_HEADS, D_K).transpose(0, 2, 1, 3)
        q, k, v = (split_heads(q), split_heads(k), split_heads(v))
        cos, sin, pair_swaps = _rope_tables(S)
        q = _apply_rope(q, cos, sin, pair_swaps)
        k = _apply_rope(k, cos, sin, pair_swaps)
        scores = jnp.einsum('bhqd,bhkd->bhqk', q, k) / math.sqrt(D_K)
        causal = jnp.tril(jnp.ones((S, S), dtype=bool))
        scores = jnp.where(causal, scores, -jnp.inf)
        probs = jax.nn.softmax(scores, axis=-1)
        ctx = jnp.einsum('bhqk,bhkd->bhqd', probs, v)
        ctx = ctx.transpose(0, 2, 1, 3).reshape(B, S, D_MODEL)
        attn_out = ctx @ wo.T
        y = x + attn_out
        h2 = _rms_norm(y, norm2_w)
        p1 = h2 @ w1.T
        p1 = p1 * jax.nn.sigmoid(p1)
        ff = p1 * (h2 @ w3.T) @ w2.T
        return y + ff

    def _L0_ffn_ref(x, w1_w, w1_s, w2_w, w2_s, h1_w, h1_s, h2_w, h2_s, w3_w, w3_s):
        import jax, jax.numpy as jnp
        import numpy as np
        D_IN, D_HID = (128, 512)

        def _ternary(key, shape):
            return jax.random.randint(key, shape, -1, 2).astype(jnp.float32)

        def _tlin(x, w, s):
            return jnp.einsum('bsi,oi->bso', x, w) * s
        h = jax.nn.silu(_tlin(x, w1_w, w1_s)) * _tlin(x, w2_w, w2_s)
        h = jax.nn.gelu(_tlin(h, h1_w, h1_s), approximate=False)
        h = jax.nn.gelu(_tlin(h, h2_w, h2_s), approximate=False)
        return _tlin(h, w3_w, w3_s)
    x = L0_attn_x
    x = x + 0.5 * _L0_ffn_ref(_layernorm(x, axis=-1), L0_ffn_w1_w, L0_ffn_w1_s, L0_ffn_w2_w, L0_ffn_w2_s, L0_ffn_h1_w, L0_ffn_h1_s, L0_ffn_h2_w, L0_ffn_h2_s, L0_ffn_w3_w, L0_ffn_w3_s)
    x = x + _L0_attn_ref(_layernorm(x, axis=-1), L0_attn_wq, L0_attn_wk, L0_attn_wv, L0_attn_wo, L0_attn_norm1_w, L0_attn_norm2_w, L0_attn_w1, L0_attn_w2, L0_attn_w3)
    x = x + 0.5 * _L0_ffn_ref(_layernorm(x, axis=-1), L0_ffn_w1_w, L0_ffn_w1_s, L0_ffn_w2_w, L0_ffn_w2_s, L0_ffn_h1_w, L0_ffn_h1_s, L0_ffn_h2_w, L0_ffn_h2_s, L0_ffn_w3_w, L0_ffn_w3_s)
    return x

_drawn_inputs = setup_inputs


def setup_inputs(seed=0):
    import zlib

    import numpy as np

    out = dict(_drawn_inputs(seed))
    spreads = {'L0_attn_norm1_w': (1.0, 0.2), 'L0_attn_norm2_w': (1.0, 0.2)}
    factors = {}
    for name, (base, spread) in spreads.items():
        noise = np.random.default_rng([zlib.crc32(name.encode()), seed]).standard_normal(out[name].shape)
        drawn = base * np.exp(spread * noise) if base else spread * noise
        out[name] = jnp.asarray(drawn.astype(out[name].dtype))
    for name, factor in factors.items():
        out[name] = (out[name] * factor).astype(out[name].dtype)
    return out
```

```python
from contextlib import ExitStack

import concourse.bass as bass
from concourse import mybir

F32 = mybir.dt.float32
F32R = mybir.dt.float32r
BF16 = mybir.dt.bfloat16
I32 = mybir.dt.int32
ALU = mybir.AluOpType
ACT = mybir.ActivationFunctionType
AX_X = mybir.AxisListType.X

P = 128
B, S, D = 8, 512, 128
NT = S // P
HID = 512
KC = HID // P
NH, DK = 16, 8
HG = 4
NG = NH // HG
EPS = 1e-5
SCALE = DK ** -0.5
MASKED = -1e30
HI, LO = 0, 1

EXACT_W = [(HI, HI), (HI, LO)]
ALL4 = [(HI, HI), (LO, HI), (LO, LO), (HI, LO)]
SPLIT3 = [(HI, HI), (LO, HI), (HI, LO)]

NE = 96
NPART = 3
M_ROW = NPART * NPART * DK


class BankPlan:

    def __init__(self, uses, banks):
        self.uses, self.banks, self.n = uses, banks, len(uses)
        self.index = {name: i for i, (name, _) in enumerate(uses)}
        assert len(self.index) == self.n
        self.per = {e: sum(r == e for _, r in uses) for e in ("act", "dve")}

    def bank(self, name):
        return self.banks[self.index[name] % len(self.banks)]

    def filled(self, it, name):
        return it * self.n + (self.index[name] + 1)

    def read(self, it, name):
        i = self.index[name]
        who = self.uses[i][1]
        return it * self.per[who] + (self.per[who] + sum(r == who for _, r in self.uses[:i + 1]))

    def last_user(self, it, name):
        i = self.index[name] % len(self.banks)
        before = [k for k in range(self.index[name]) if k % len(self.banks) == i]
        if before:
            k = before[-1]
            return self.uses[k][1], self.read(it, self.uses[k][0])
        k = [k for k in range(self.n) if k % len(self.banks) == i][-1]
        who = self.uses[k][1]
        return who, it * self.per[who] + sum(r == who for _, r in self.uses[:k + 1])


def ffn_uses():
    uses = []
    for j in range(2):
        for c in range(KC):
            uses += [(("a", j, c), "act"), (("u", j, c), "dve")]
    for layer in ("h1", "h2"):
        uses += [((layer, j, c), "act") for j in range(2) for c in range(KC)]
    uses += [(("y", j), "act") for j in range(2)]
    uses += [(("yT", j), "dve") for j in range(2)]
    return uses


def inner_ffn_uses():
    def first(j, chunks):
        return [use for c in chunks for use in ((("ia", j, c), "act"), (("iu", j, c), "dve"))]

    return (first(0, range(KC)) + first(1, range(2)) + [(("iy", 0), "act")] + first(1, [2])
            + [(("iyT", 0), "dve")] + first(1, [3]) + [(("iy", 1), "act"), (("iyT", 1), "dve")])


RING8 = list(range(6))
T_BANK = 6


def product(pe, out, weights, data, chunks, parts):
    order = [(k, w, d) for k in range(chunks) for w, d in parts]
    for n, (k, w, d) in enumerate(order):
        last = pe.matmul(out, weights(k, w), data(k, d), start=(n == 0), stop=(n == len(order) - 1))
    return last


class Ffn:

    NSLOT = 4

    def __init__(self, nc, sb, sem, psum, constants, weights, plan, inner):
        self.nc, self.psum, self.plan = nc, psum, plan
        self.w, self.fw = constants, weights
        self.xn = sb("xn", [P, 2, NT, D], F32)
        self.xT = sb("xT", [P, 2, 2, S], F32R)
        self.g = sb("g", [P, self.NSLOT, S], F32)
        self.hf = sb("hf", [P, self.NSLOT, S], F32)
        self.H = sb("H", [P, 2, 2, KC, 2, S], F32R)
        self.yT = sb("yT", [P, 2, S], F32)
        self.stats = sb("stats", [P, 2, NT, 6], F32)
        self.mv = sb("mv", [P, 2, NT, 2], F32)
        self.var = sb("var", [P, 2, NT], F32)
        self.rstd = sb("rstd", [P, 2, NT], F32)
        self.spare = sb("spare", [P, 4], F32)
        self.filled = sem("banks_filled")
        self.act_read, self.dve_read = sem("act_read"), sem("dve_read")
        self.hi_ready, self.lo_ready = sem("hi_ready"), sem("lo_ready")
        self.xn_ready, self.xT_hi = sem("xn_ready"), sem("xT_hi")
        self.xT_filled, self.xT_read = sem("xT_filled"), sem("xT_read")
        self.stats_ready, self.moments = sem("stats_ready"), sem("moments")
        self.pool_step, self.rstd_ready = sem("pool_step"), sem("rstd_ready")
        self.first = 2 * KC if inner else 0
        self.per = self.first + 6 * KC
        self.norms = 2 if inner else 1

    def read_sem(self, who):
        return self.act_read if who == "act" else self.dve_read

    def slot(self, layer, j, c):
        base = {"ia": 0, "a": self.first, "h1": self.first + 2 * KC, "h2": self.first + 4 * KC}[layer]
        return base + KC * j + c

    def bank(self, name):
        return self.psum[:, self.plan.bank(name), :]

    def norm_count(self, it, which, j):
        return (it * self.norms + which) * 2 + (j + 1)

    def pool_rstd(self, pool, it, which, j, mean_square):
        n = self.norm_count(it, which, j)
        pool.wait_ge(self.moments, n)
        steps = (n - 1) * 3
        if mean_square:
            self.nc.gpsimd.tensor_tensor(self.rstd[:, j], self.mv[:, j, :, 0], self.mv[:, j, :, 0],
                                         ALU.mult).then_inc(self.pool_step, 1)
            pool.wait_ge(self.pool_step, steps + 1)
            self.nc.gpsimd.tensor_tensor(self.var[:, j], self.mv[:, j, :, 1], self.rstd[:, j],
                                         ALU.add).then_inc(self.pool_step, 1)
            pool.wait_ge(self.pool_step, steps + 2)
            self.nc.gpsimd.tensor_tensor(self.var[:, j], self.var[:, j], self.w.eps[:, :],
                                         ALU.add).then_inc(self.pool_step, 1)
        else:
            self.nc.gpsimd.tensor_tensor(self.var[:, j], self.mv[:, j, :, 1], self.w.eps[:, :],
                                         ALU.add).then_inc(self.pool_step, 3)
        pool.wait_ge(self.pool_step, steps + 3)
        self.nc.gpsimd.tensor_tensor(self.rstd[:, j], self.var[:, j], self.w.minus_half[:, 0:NT],
                                     ALU.pow).then_inc(self.rstd_ready, 1)

    def dve_moments(self, dve, j, src):
        for i in range(NT):
            last = self.nc.vector.bn_stats(self.stats[:, j, i], src[:, i, :])
        last.then_inc(self.stats_ready, 1)

    def dve_aggregate(self, dve, j):
        for i in range(NT):
            last = self.nc.vector.bn_aggr(self.mv[:, j, i], self.stats[:, j, i])
        last.then_inc(self.moments, 1)

    def dve_normalise(self, dve, it, which, j, src, subtract_mean):
        n = self.norm_count(it, which, j)
        dve.wait_ge(self.rstd_ready, n)
        for i in range(NT):
            if subtract_mean:
                last = self.nc.vector.tensor_scalar(self.xn[:, j, i], src[:, i, :], self.mv[:, j, i, 0:1],
                                                    self.rstd[:, j, i:i + 1], ALU.subtract, ALU.mult)
            else:
                last = self.nc.vector.tensor_scalar(self.xn[:, j, i], src[:, i, :],
                                                    self.rstd[:, j, i:i + 1], None, ALU.mult)
        last.then_inc(self.xn_ready, 1)

    def dve_split_xT(self, dve, it, which, j, weight):
        n = self.norm_count(it, which, j)
        dve.wait_ge(self.xT_filled, n)
        bank = self.psum[:, T_BANK + j, :]
        if weight is None:
            self.nc.vector.tensor_copy(self.xT[:, j, HI], bank).then_inc(self.xT_hi, 1)
            dve.wait_ge(self.xT_hi, n)
            self.nc.vector.tensor_tensor(self.xT[:, j, LO], bank, self.xT[:, j, HI].bitcast(F32),
                                         ALU.subtract).then_inc(self.xT_read, 1)
        else:
            self.nc.vector.tensor_scalar(self.xT[:, j, HI], bank, weight, None,
                                         ALU.mult).then_inc(self.xT_hi, 1)
            dve.wait_ge(self.xT_hi, n)
            self.nc.vector.scalar_tensor_tensor(self.xT[:, j, LO], bank, weight, self.xT[:, j, HI].bitcast(F32),
                                                ALU.mult, ALU.subtract).then_inc(self.xT_read, 1)

    def pe_bank(self, pe, it, name):
        who, value = self.plan.last_user(it, name)
        pe.wait_ge(self.read_sem(who), value)
        return self.bank(name)

    def pe_transpose_in(self, pe, it, which, j):
        n = self.norm_count(it, which, j)
        bank = self.psum[:, T_BANK + j, :]
        pe.wait_ge(self.xT_read, n)
        pe.wait_ge(self.xn_ready, n)
        for i in range(NT):
            last = pe.transpose(bank[:, i * P:(i + 1) * P], self.xn[:, j, i, :], self.w.ident[:, :])
        last.then_inc(self.xT_filled, 1)

    def pe_first(self, pe, it, which, j, names, weights, parts, chunks=range(KC)):
        pe.wait_ge(self.xT_read, self.norm_count(it, which, j) + 2)
        for c in chunks:
            for name, w in zip(names, weights):
                bank = self.pe_bank(pe, it, (name, j, c))
                product(pe, bank, lambda k, p: w[:, p, c * P:(c + 1) * P],
                        lambda k, p: self.xT[:, j, p], 1, parts).then_inc(self.filled, 1)

    def pe_hidden(self, pe, it, j, layer, before, w, src, parts):
        for c in range(KC):
            bank = self.pe_bank(pe, it, (layer, j, c))
            order = [(k, wp, dp) for k in range(KC) for wp, dp in parts]
            for n, (k, wp, dp) in enumerate(order):
                if c == 0 and n % len(parts) == 0:
                    pe.wait_ge(self.lo_ready, it * self.per + self.slot(before, j, k) + 1)
                last = pe.matmul(bank, w[:, wp, k, c * P:(c + 1) * P], self.H[:, j, src, k, dp],
                                 start=(n == 0), stop=(n == len(order) - 1))
            last.then_inc(self.filled, 1)

    def pe_out(self, pe, it, j, name, before, w, src, parts):
        bank = self.pe_bank(pe, it, (name, j))
        order = [(k, wp, dp) for k in range(KC) for wp, dp in parts]
        for n, (k, wp, dp) in enumerate(order):
            if n % len(parts) == 0:
                pe.wait_ge(self.lo_ready, it * self.per + self.slot(before, j, k) + 1)
            last = pe.matmul(bank, w[:, wp, k, :], self.H[:, j, src, k, dp],
                             start=(n == 0), stop=(n == len(order) - 1))
        last.then_inc(self.filled, 1)

    def pe_transpose_out(self, pe, it, j, name, yname):
        bank = self.pe_bank(pe, it, (name, j))
        pe.wait_ge(self.act_read, self.plan.read(it, (yname, j)))
        for i in range(NT):
            last = pe.transpose(bank[:, i * P:(i + 1) * P], self.yT[:, j, i * P:(i + 1) * P], self.w.ident[:, :])
        last.then_inc(self.filled, 1)

    def act_slot_free(self, act, it, idx):
        if idx >= self.NSLOT:
            act.wait_ge(self.lo_ready, it * self.per + (idx - self.NSLOT + 1))

    def act_first(self, act, it, j, aname, scale, dst, steps=range(KC + 1)):
        for c in steps:
            if c < KC:
                idx = self.slot(aname, j, c)
                self.act_slot_free(act, it, idx)
                act.wait_ge(self.filled, self.plan.filled(it, (aname, j, c)))
                kw = {} if scale is None else {"scale": scale[:, c:c + 1]}
                act.activation(self.g[:, idx % self.NSLOT], self.bank((aname, j, c)), ACT.Silu,
                               **kw).then_inc(self.act_read, 1)
            if c > 0:
                idx = self.slot(aname, j, c - 1)
                uname = "iu" if aname == "ia" else "u"
                act.wait_ge(self.dve_read, self.plan.read(it, (uname, j, c - 1)))
                act.activation(self.H[:, j, dst, c - 1, HI], self.hf[:, idx % self.NSLOT],
                               ACT.Copy).then_inc(self.hi_ready, 1)

    def act_hidden(self, act, it, j, layer, scale, dst):
        for c in range(KC):
            idx = self.slot(layer, j, c)
            act.wait_ge(self.filled, self.plan.filled(it, (layer, j, c)))
            act.activation(self.H[:, j, dst, c, HI], self.bank((layer, j, c)), ACT.Gelu,
                           scale=scale[:, c:c + 1]).then_inc(self.hi_ready, 1)
            self.act_slot_free(act, it, idx)
            act.activation(self.g[:, idx % self.NSLOT], self.bank((layer, j, c)), ACT.Gelu,
                           scale=scale[:, c:c + 1]).then_inc(self.act_read, 1)

    def act_out(self, act, it, j, name, scale):
        act.wait_ge(self.filled, self.plan.filled(it, (name, j)))
        kw = {} if scale is None else {"scale": scale}
        act.activation(self.yT[:, j], self.bank((name, j)), ACT.Copy, **kw).then_inc(self.act_read, 1)

    def dve_first(self, dve, it, j, aname, uname, scale, dst, steps=range(KC + 1)):
        for c in steps:
            if c < KC:
                idx = self.slot(aname, j, c)
                if idx >= self.NSLOT:
                    dve.wait_ge(self.lo_ready, it * self.per + idx - self.NSLOT + 1)
                dve.wait_ge(self.act_read, self.plan.read(it, (aname, j, c)))
                dve.wait_ge(self.filled, self.plan.filled(it, (uname, j, c)))
                slot = idx % self.NSLOT
                s = 1.0 if scale is None else scale[:, c:c + 1]
                self.nc.vector.scalar_tensor_tensor(self.hf[:, slot], self.bank((uname, j, c)), s, self.g[:, slot],
                                                    ALU.mult, ALU.mult).then_inc(self.dve_read, 1)
            if c > 0:
                idx = self.slot(aname, j, c - 1)
                dve.wait_ge(self.hi_ready, it * self.per + idx + 1)
                self.nc.vector.tensor_tensor(self.H[:, j, dst, c - 1, LO], self.hf[:, idx % self.NSLOT],
                                             self.H[:, j, dst, c - 1, HI].bitcast(F32),
                                             ALU.subtract).then_inc(self.lo_ready, 1)

    def dve_hidden(self, dve, it, j, layer, dst):
        for c in range(KC):
            idx = self.slot(layer, j, c)
            dve.wait_ge(self.act_read, self.plan.read(it, (layer, j, c)))
            self.nc.vector.tensor_tensor(self.H[:, j, dst, c, LO], self.g[:, idx % self.NSLOT],
                                         self.H[:, j, dst, c, HI].bitcast(F32),
                                         ALU.subtract).then_inc(self.lo_ready, 1)

    def dve_add(self, dve, it, j, name, x):
        dve.wait_ge(self.filled, self.plan.filled(it, (name, j)))
        self.nc.vector.tensor_tensor(x, x, self.bank((name, j)), ALU.add).then_inc(self.dve_read, 1)

    def pe_outer_first(self, pe, it, j, parts):
        which = self.norms - 1
        self.pe_first(pe, it, which, j, ("a", "u"), (self.fw.w1, self.fw.w2), parts)

    def pe_outer_rest(self, pe, it, parts, following):
        w = self.fw
        for j in range(2):
            self.pe_hidden(pe, it, j, "h1", "a", w.h1, 0, parts)
        for j in range(2):
            self.pe_hidden(pe, it, j, "h2", "h1", w.h2, 1, parts)
        if following is not None:
            for j in range(2):
                self.pe_transpose_in(pe, following, 0, j)
        for j in range(2):
            self.pe_out(pe, it, j, "y", "h2", w.w3, 0, parts)
        for j in range(2):
            self.pe_transpose_out(pe, it, j, "yT", "y")

    def dve_outer_rest(self, dve, it, x, following, src, weight, subtract_mean):
        if following is not None:
            for j in range(2):
                self.dve_moments(dve, j, src[:, following * 2 + j])
        self.dve_hidden(dve, it, 0, "h1", 1)
        if following is not None:
            dve.wait_ge(self.stats_ready, self.norm_count(following, 0, 1))
        self.dve_hidden(dve, it, 1, "h1", 1)
        if following is not None:
            for j in range(2):
                self.dve_aggregate(dve, j)
        self.dve_hidden(dve, it, 0, "h2", 0)
        if following is not None:
            for j in range(2):
                self.dve_normalise(dve, following, 0, j, src[:, following * 2 + j], subtract_mean)
        self.dve_hidden(dve, it, 1, "h2", 0)
        if following is not None:
            for j in range(2):
                self.dve_split_xT(dve, following, 0, j, weight)
        for j in range(2):
            self.dve_add(dve, it, j, "yT", x[:, it * 2 + j].rearrange("p i d -> p (i d)"))

    def act_outer(self, act, it):
        w = self.w
        for j in range(2):
            self.act_first(act, it, j, "a", w.scale[:, 0], 0)
        for j in range(2):
            self.act_hidden(act, it, j, "h1", w.scale[:, 2], 1)
        for j in range(2):
            self.act_hidden(act, it, j, "h2", w.scale[:, 3], 0)
        for j in range(2):
            self.act_out(act, it, j, "y", w.half_s3[:, 0:1])



def max_units(g):
    per_bank = {0: 4, 1: 2, 2: 1, 3: 1}
    return [(i, h, per_bank[i]) for i in range(NT) for h in range(0, HG, per_bank[i])]


CUTS = (1, 3, 0, 7)
TAIL = (1, 4, 1, 1, 2, 2)


def cut_units(g, cuts, lo, hi):
    return max_units(g)[sum(cuts[:lo]):sum(cuts[:hi])]


def prologue_uses():
    return ([(("hT",), "dve")] + [(("qkv", i), "dve") for i in range(NT)] + [(("qkT", n), "dve") for n in range(2)]
            + [(("max", 0, u), "dve") for u in max_units(0)] + [(("mT", 0), "act")]
            + [(("max", 1, u), "dve") for u in max_units(1)] + [(("mT", 1), "act")])


def attention_uses(last):
    def maxima(g, units):
        return [(("max", g, u), "dve") for u in units]

    def following(uses):
        return [] if last else uses

    uses = following([(("hT",), "dve")] + [(("qkv", i), "dve") for i in range(NT)]
                     + [(("qkT", n), "dve") for n in range(2)])
    uses += maxima(2, max_units(2))
    uses += maxima(3, cut_units(3, CUTS, 0, 1)) + [(("mT", 2), "act")]
    uses += maxima(3, cut_units(3, CUTS, 1, 3)) + [(("ctxT", 0), "dve")] + maxima(3, cut_units(3, CUTS, 3, 4))
    uses += following(maxima(0, cut_units(0, CUTS, 0, 1))) + [(("mT", 3), "act")]
    uses += following(maxima(0, cut_units(0, CUTS, 1, 3))) + [(("ctxT", 1), "dve")]
    uses += following(maxima(0, cut_units(0, CUTS, 3, 4)))
    uses += following(maxima(1, cut_units(1, TAIL, 0, 1)) + [(("mT", 0), "act")])
    uses += following(maxima(1, cut_units(1, TAIL, 1, 3))) + [(("ctxT", 2), "dve")]
    uses += following(maxima(1, cut_units(1, TAIL, 3, 4))) + [(("ctxT", 3), "dve")]
    uses += following(maxima(1, cut_units(1, TAIL, 4, 5))) + [(("cT",), "dve")]
    uses += following(maxima(1, cut_units(1, TAIL, 5, 6))) + [(("wo",), "act")]
    uses += following([(("mT", 1), "act")]) + [(("attn",), "dve")]
    return uses


RING = [4, 5, 6]
CTX_BANK = 7
MASK_STEPS = 8
UNITS = 5
NV = 16
EXT_DMAS = 2 * NPART * NPART + 1


class AttentionBuffers:
    def __init__(self, sb):
        self.wa = sb("wa", [P, 2, 4 * D], F32R)
        self.hn = sb("hn", [P, NT, D], F32)
        self.hT = sb("hT", [P, 2, S], F32R)
        self.stats = sb("stats", [P, NT, 6], F32)
        self.mv = sb("mv", [P, NT, 2], F32)
        self.small = sb("small", [P, 4, NT], F32)
        self.rstd = sb("rstd", [P, NT], F32)
        self.both = sb("both", [P, NT], F32)
        self.cos_part = sb("cos_part", [P, 2, 2 * D], F32)
        self.sin_part = sb("sin_part", [P, 2, 2 * D], F32)
        self.qk = sb("qk", [P, NT, 2, DK, NH], F32)
        self.part = sb("part", [P, 2, NPART, S], BF16)
        self.rest = sb("rest", [P, 2, S], F32)
        self.ext = [[sb(f"{n}_ext{p}", [NE, NH, S], BF16) for n in ("q", "k")] for p in range(2)]
        self.V = [sb(f"V{p}", [P, NT, NH, NV], F32) for p in range(2)]
        self.zero = sb("zero", [P, 1], F32)
        self.spare = sb("spare", [P, 1], F32)
        self.neg_max = sb("neg_max", [P, 2, NT, HG], F32)
        self.neg_max2 = sb("neg_max2", [P, NT, 2, HG], BF16)
        self.max_rows = sb("max_rows", [2 * HG, S], BF16)
        self.PT = sb("PT", [P, 2, UNITS, 2 * S], F32)
        self.ctxs = sb("ctxs", [P, 2, S], F32)
        self.recip = sb("recip", [P, 2, NT, HG], F32)
        self.ctxn = sb("ctxn", [P, NT, NH, DK], F32)
        self.cT = sb("cT", [P, 2, S], F32R)
        self.aT = sb("aT", [P, S], F32)
        self.ident16 = sb("ident16", [P, P], BF16)
        self.mask16 = sb("mask16", [P, P], BF16)
        self.fill16 = sb("fill16", [P, 2, P], BF16)
        self.tab = sb("tab", [P, 2, NT, DK], F32)


class Attention:

    def __init__(self, nc, bufs, psum, w, x, y2, plan, sem, shared, first):
        self.nc, self.t, self.psum, self.w, self.x, self.y2, self.plan = nc, bufs, psum, w, x, y2, plan
        self.first = first
        self.ext_loaded, self.m_loaded = shared
        self.s_filled = sem("filled")
        self.s_act_read = sem("act_read")
        self.s_dve_read = sem("dve_read")
        self.s_stats_ready = sem("stats_ready")
        self.s_moments = sem("moments")
        self.s_pool_step = sem("pool_step")
        self.s_factors = sem("factors")
        self.s_hn_ready = sem("hn_ready")
        self.s_hT_hi = sem("hT_hi")
        self.s_rope_step = sem("rope_step")
        self.s_qk_hi = sem("qk_hi")
        self.s_mid_ready = sem("mid_ready")
        self.s_parts_ready = sem("parts_ready")
        self.s_max_hi = sem("max_hi")
        self.s_max_ready = sem("max_ready")
        self.s_scores = sem("scores")
        self.s_exps = sem("exps")
        self.s_masks = sem("masks")
        self.s_ctx = sem("ctx")
        self.s_ctx_read = sem("ctx_read")
        self.s_recips = sem("recips")
        self.s_cT_hi = sem("cT_hi")
        self.s_x_done = sem("x_done")

    def bank(self, name):
        return self.psum[:, self.plan.bank(name), :]

    def pe_bank(self, pe, b, name):
        who, value = self.plan.last_user(b, name)
        pe.wait_ge(self.s_act_read if who == "act" else self.s_dve_read, value)
        return self.bank(name)

    def dve_moments(self, dve, b, s):
        for i in range(NT):
            last = self.nc.vector.bn_stats(self.t.stats[:, i], self.x[:, s, i, :])
        last.then_inc(self.s_stats_ready, 1)

    def dve_aggregate(self, dve, b):
        for i in range(NT):
            last = self.nc.vector.bn_aggr(self.t.mv[:, i], self.t.stats[:, i])
        last.then_inc(self.s_moments, 1)

    def pool_factors(self, pool, b):
        t, g, n = self.t, self.nc.gpsimd, 6
        pool.wait_ge(self.s_moments, b + 1)
        var = t.mv[:, :, 1]
        g.tensor_tensor(t.small[:, 0], var, self.w.eps[:, :], ALU.add).then_inc(self.s_pool_step, 1)
        pool.wait_ge(self.s_pool_step, b * n + 1)
        g.tensor_tensor(t.rstd[:, :], t.small[:, 0], self.w.minus_half[:, :], ALU.pow).then_inc(self.s_pool_step, 1)
        pool.wait_ge(self.s_pool_step, b * n + 2)
        g.tensor_tensor(t.small[:, 1], var, t.rstd[:, :], ALU.mult).then_inc(self.s_pool_step, 1)
        pool.wait_ge(self.s_pool_step, b * n + 3)
        g.tensor_tensor(t.small[:, 2], t.small[:, 1], t.rstd[:, :], ALU.mult).then_inc(self.s_pool_step, 1)
        pool.wait_ge(self.s_pool_step, b * n + 4)
        g.tensor_tensor(t.small[:, 1], t.small[:, 2], self.w.eps[:, :], ALU.add).then_inc(self.s_pool_step, 1)
        pool.wait_ge(self.s_pool_step, b * n + 5)
        g.tensor_tensor(t.small[:, 3], t.small[:, 1], self.w.minus_half[:, :], ALU.pow).then_inc(self.s_pool_step, 1)
        pool.wait_ge(self.s_pool_step, b * n + 6)
        g.tensor_tensor(t.both[:, :], t.small[:, 3], t.rstd[:, :], ALU.mult).then_inc(self.s_factors, 1)

    def dve_normalise(self, dve, b, s):
        t = self.t
        dve.wait_ge(self.s_factors, b + 1)
        for i in range(NT):
            last = self.nc.vector.tensor_scalar(t.hn[:, i], self.x[:, s, i, :], t.mv[:, i, 0:1], t.both[:, i:i + 1],
                                                ALU.subtract, ALU.mult)
        last.then_inc(self.s_hn_ready, 1)

    def dve_layernorm(self, dve, b, s):
        t = self.t
        for i in range(NT):
            self.nc.vector.tensor_scalar(self.y2[:, s, i, :], self.x[:, s, i, :], t.mv[:, i, 0:1],
                                         t.rstd[:, i:i + 1], ALU.subtract, ALU.mult)

    def pe_hT(self, pe, b):
        bank = self.pe_bank(pe, b, ("hT",))
        pe.wait_ge(self.s_hn_ready, b + 1)
        for i in range(NT):
            last = pe.transpose(bank[:, i * P:(i + 1) * P], self.t.hn[:, i, :], self.w.ident[:, :])
        last.then_inc(self.s_filled, 1)

    def act_hT(self, act, b):
        act.wait_ge(self.s_filled, self.plan.filled(b, ("hT",)))
        act.activation(self.t.hT[:, HI], self.bank(("hT",)), ACT.Copy,
                       scale=self.w.norms[:, 0:1]).then_inc(self.s_hT_hi, 1)

    def dve_hT(self, dve, b):
        t, bank, weight = self.t, self.bank(("hT",)), self.w.norms[:, 0:1]
        dve.wait_ge(self.s_hT_hi, b + 1)
        self.nc.vector.scalar_tensor_tensor(t.hT[:, LO], bank, weight, t.hT[:, HI].bitcast(F32), ALU.mult,
                                            ALU.subtract).then_inc(self.s_dve_read, 1)

    def pe_qkv(self, pe, b, i):
        t = self.t
        if i == 0:
            pe.wait_ge(self.s_dve_read, self.plan.read(b, ("hT",)))
        bank = self.pe_bank(pe, b, ("qkv", i))
        for n, (wp, dp) in enumerate(SPLIT3):
            last = pe.matmul(bank[:, 0:3 * D], t.hT[:, dp, i * P:(i + 1) * P], t.wa[:, wp, 0:3 * D],
                             start=(n == 0), stop=(n == len(SPLIT3) - 1))
        last.then_inc(self.s_filled, 1)

    def dve_rope(self, dve, b, par):
        t, v = self.t, self.nc.vector
        for i in range(NT):
            bank, slot = self.bank(("qkv", i)), i % 2
            qk = bank[:, 0:2 * D].rearrange("p (n d) -> p n d", d=DK)
            dve.wait_ge(self.s_filled, self.plan.filled(b, ("qkv", i)))
            if i >= 2:
                dve.wait_ge(self.s_dve_read, self.plan.read(b, ("qkv", i - 2)))
            cos = t.tab[:, 0, i:i + 1, :].to_broadcast([P, 2 * NH, DK])
            v.tensor_tensor(t.cos_part[:, slot].rearrange("p (n d) -> p n d", d=DK), qk, cos, ALU.mult)
            sin = t.tab[:, 1, i:i + 1, :].to_broadcast([P, 2 * NH, DK]).rearrange("p n (d e) -> p n d e", e=2)
            swapped = t.sin_part[:, slot].rearrange("p (n d e) -> p n d e", d=DK // 2, e=2)
            v.tensor_tensor(swapped[:, :, :, ::-1],
                            bank[:, 0:2 * D].rearrange("p (n d e) -> p n d e", d=DK // 2, e=2), sin,
                            ALU.mult).then_inc(self.s_rope_step, 1)
            dve.wait_ge(self.s_rope_step, b * NT + (i + 1))
            v.tensor_tensor(t.qk[:, i].rearrange("p q d h -> p q h d"),
                            t.cos_part[:, slot].rearrange("p (q h d) -> p q h d", q=2, d=DK),
                            t.sin_part[:, slot].rearrange("p (q h d) -> p q h d", q=2, d=DK), ALU.add)
            v.tensor_copy(t.V[par][:, i, :, 0:DK],
                          bank[:, 2 * D:3 * D].rearrange("p (h d) -> p h d", d=DK)).then_inc(self.s_dve_read, 1)

    def pe_qkT(self, pe, b):
        for n in range(2):
            bank = self.pe_bank(pe, b, ("qkT", n))
            pe.wait_ge(self.s_dve_read, self.plan.read(b, ("qkv", NT - 1)))
            for i in range(NT):
                last = pe.transpose(bank[:, i * P:(i + 1) * P],
                                    self.t.qk[:, i, n].rearrange("p d h -> p (d h)"), self.w.ident[:, :])
            last.then_inc(self.s_filled, 1)

    def act_qkT(self, act, b, loads_before):
        for n in range(2):
            act.wait_ge(self.s_filled, self.plan.filled(b, ("qkT", n)))
            if loads_before is not None:
                act.wait_ge(self.ext_loaded, loads_before)
            act.activation(self.t.part[:, n, 0], self.bank(("qkT", n)), ACT.Copy).then_inc(self.s_qk_hi, 1)

    def dve_rest(self, dve, b):
        for n in range(2):
            dve.wait_ge(self.s_qk_hi, b * 2 + (n + 1))
            self.nc.vector.tensor_tensor(self.t.rest[:, n], self.bank(("qkT", n)), self.t.part[:, n, 0],
                                         ALU.subtract).then_inc(self.s_dve_read, 1)

    def act_parts(self, act, b, n):
        act.wait_ge(self.s_dve_read, self.plan.read(b, ("qkT", n)))
        act.activation(self.t.part[:, n, 1], self.t.rest[:, n], ACT.Copy).then_inc(self.s_mid_ready, 1)

    def pool_parts(self, pool, b):
        t = self.t
        for n in range(2):
            pool.wait_ge(self.s_mid_ready, b * 2 + (n + 1))
            self.nc.gpsimd.tensor_tensor(t.part[:, n, 2], t.rest[:, n], t.part[:, n, 1],
                                         ALU.subtract).then_inc(self.s_parts_ready, 1)

    def sp_ext(self, sp, b, par):
        t = self.t
        for n in range(2):
            sp.wait_ge(self.s_parts_ready, b * 2 + (n + 1))
            for a in range(NPART):
                for c in range(NPART):
                    row = DK * (NPART * a + c)
                    part = t.part[:, n, c if n == 0 else a, :]
                    sp.dma_start(t.ext[par][n][row:row + DK, :, :], part).then_inc(self.ext_loaded, 16)
            if n == 0:
                sp.dma_start(t.ext[par][0][M_ROW:M_ROW + 2, :, :], t.fill16[:, 0, :]).then_inc(self.ext_loaded, 16)

    def pe_max(self, pe, b, g, par, loads, units=None):
        t = self.t
        q_ext, k_ext = t.ext[par]
        if loads is not None:
            pe.wait_ge(self.ext_loaded, loads)
        for unit in max_units(g) if units is None else units:
            i, h0, nh = unit
            bank, width = self.pe_bank(pe, b, ("max", g, unit)), (i + 1) * P
            for k in range(nh):
                h = HG * g + h0 + k
                pe.matmul(bank[:, k * width:(k + 1) * width], q_ext[:, h, i * P:(i + 1) * P], k_ext[:, h, 0:width],
                          start=True, stop=False)
                last = pe.matmul(bank[:, k * width + i * P:(k + 1) * width], t.ident16[:, :], t.mask16[:, :],
                                 start=False, stop=True)
            last.then_inc(self.s_filled, 1)

    def dve_max(self, dve, b, g, units=None):
        t = self.t
        for unit in max_units(g) if units is None else units:
            i, h0, nh = unit
            dve.wait_ge(self.s_filled, self.plan.filled(b, ("max", g, unit)))
            scores = self.bank(("max", g, unit))[:, 0:nh * (i + 1) * P].rearrange("p (h k) -> p h k", h=nh)
            self.nc.vector.tensor_reduce(t.neg_max[:, g % 2, i, h0:h0 + nh], scores, AX_X, ALU.max,
                                         negate=True).then_inc(self.s_dve_read, 1)

    def dve_max_parts(self, dve, b, g, slot):
        t, v = self.t, self.nc.vector
        n = b * NG + slot
        dve.wait_ge(self.s_dve_read, self.plan.read(b, ("max", g, max_units(g)[-1])))
        v.tensor_copy(t.neg_max2[:, :, 0], t.neg_max[:, g % 2]).then_inc(self.s_max_hi, 1)
        dve.wait_ge(self.s_max_hi, n + 1)
        v.tensor_tensor(t.neg_max2[:, :, 1], t.neg_max[:, g % 2], t.neg_max2[:, :, 0],
                        ALU.subtract).then_inc(self.s_max_ready, 1)

    def pe_mT(self, pe, b, g, slot):
        bank = self.pe_bank(pe, b, ("mT", g)).bitcast(BF16)
        pe.wait_ge(self.s_max_ready, b * NG + (slot + 1))
        for i in range(NT):
            last = pe.transpose(bank[0:2 * HG, i * P:(i + 1) * P],
                                self.t.neg_max2[:, i].rearrange("p n h -> p (n h)"), self.t.ident16[:, :])
        last.then_inc(self.s_filled, 1)

    def act_mT(self, act, b, g, loaded_before, par):
        act.wait_ge(self.s_filled, self.plan.filled(b, ("mT", g)))
        if loaded_before is not None:
            act.wait_ge(self.m_loaded, loaded_before)
        act.activation(self.t.max_rows[:, :], self.bank(("mT", g)).bitcast(BF16)[0:2 * HG, 0:S],
                       ACT.Copy).then_inc(self.s_act_read, 1)
        act.wait_ge(self.s_act_read, self.plan.read(b, ("mT", g)))
        for n in range(2):
            act.dma_start(self.t.ext[par][0][M_ROW + n:M_ROW + n + 1, HG * g:HG * (g + 1), :],
                          self.t.max_rows[n * HG:(n + 1) * HG, :]).then_inc(self.m_loaded, 16)

    def pieces(self, u):
        if u < HG:
            return [(u, 0, 0), (u, 1, S), (u, 3, S + 3 * P)]
        return [(h, 2, h * 2 * P) for h in range(HG)]

    def pe_scores(self, pe, b, g, par, units=range(UNITS)):
        q_ext, k_ext = self.t.ext[par]
        pe.wait_ge(self.m_loaded, (b + self.first) * (NG * 32) + (g + 1) * 32)
        for u in units:
            n = UNITS * g + u
            pe.wait_ge(self.s_exps, b * (NG * UNITS) + (n + 1))
            both = self.psum[:, 2 * (n % 2):2 * (n % 2) + 2, :].rearrange("p n s -> p (n s)")
            for h, j, col in self.pieces(u):
                width = S - j * P
                last = pe.matmul(both[:, col:col + width], k_ext[:, HG * g + h, j * P:(j + 1) * P],
                                 q_ext[:, HG * g + h, j * P:S], start=True, stop=True)
            last.then_inc(self.s_scores, 1)

    def act_exp(self, act, b, g, units=range(UNITS)):
        t = self.t
        for u in units:
            n = UNITS * g + u
            if u == 0:
                act.wait_ge(self.s_ctx, b * NG + (g + 3))
            act.wait_ge(self.s_scores, b * (NG * UNITS) + (n + 1))
            act.activation(t.PT[:, g % 2, u], self.psum[:, 2 * (n % 2):2 * (n % 2) + 2, :].rearrange("p n s -> p (n s)"),
                           ACT.Exp, scale=SCALE).then_inc(self.s_exps, 1)

    def pool_mask(self, pool, b, g):
        t = self.t
        heads = t.PT[:, g % 2, 0:HG, :].rearrange("p h (n q) -> p h n q", q=P)
        third = t.PT[:, g % 2, HG, :].rearrange("p (h q) -> p h q", h=HG)[:, :, 0:P]
        stages = [(2, [heads[:, 0:2, 0:2 * NT:NT, :], heads[:, 0:2, 2 * NT - 1, :]]),
                  (4, [heads[:, 2:4, 0:2 * NT:NT, :], heads[:, 2:4, 2 * NT - 1, :]]), (5, [third])]
        n = b * (NG * MASK_STEPS) + MASK_STEPS * g + 1
        for units, views in stages:
            pool.wait_ge(self.s_exps, b * (NG * UNITS) + (UNITS * g + units + 2))
            pool.wait_ge(self.s_masks, n)
            self.nc.gpsimd.tensor_tensor(t.spare[:, :], t.zero[:, :], t.zero[:, :],
                                         ALU.add).then_inc(self.s_masks, 1)
            for v in views:
                repeated = [[0, k] for k in v.shape[1:-1]]
                self.nc.gpsimd.affine_select(out=v, in_=v, compare_op=ALU.is_ge, fill=0.0, base=0,
                                             pattern=repeated + [[1, P]], channel_multiplier=-1).then_inc(self.s_masks, 1)
            n = n + (1 + len(views))

    def pe_context(self, pe, b, g, par, j):
        t = self.t
        if j == 0:
            pe.wait_ge(self.s_masks, b * (NG * MASK_STEPS) + (MASK_STEPS * (g + 1) + 1))
            pe.wait_ge(self.s_ctx_read, b * NG + (g + 1))
        for h in range(HG):
            unit, col = {0: (h, 0), 1: (h, S), 3: (h, S + 3 * P), 2: (HG, h * 2 * P)}[j]
            last = pe.matmul(self.psum[32 * h:32 * h + NV, CTX_BANK, j * P:S], t.V[par][:, j, HG * g + h, :],
                             t.PT[:, g % 2, unit, col:col + S - j * P], start=(j == 0), stop=(j == NT - 1))
        if j == NT - 1:
            last.then_inc(self.s_ctx, 1)

    def act_context(self, act, b, g):
        act.wait_ge(self.s_ctx, b * NG + (g + 5))
        act.activation(self.t.ctxs[:, g % 2], self.psum[:, CTX_BANK, :], ACT.Copy).then_inc(self.s_ctx_read, 1)

    def pe_ctxT(self, pe, b, g):
        bank = self.pe_bank(pe, b, ("ctxT", g))
        pe.wait_ge(self.s_ctx_read, b * NG + (g + 2))
        for i in range(NT):
            last = pe.transpose(bank[:, i * P:(i + 1) * P], self.t.ctxs[:, g % 2, i * P:(i + 1) * P], self.w.ident[:, :])
        last.then_inc(self.s_filled, 1)

    def dve_ctxT(self, dve, b, g):
        t, v = self.t, self.nc.vector
        ctx = self.bank(("ctxT", g)).rearrange("p (i h c) -> p i h c", i=NT, h=HG)
        dve.wait_ge(self.s_filled, self.plan.filled(b, ("ctxT", g)))
        v.reciprocal(t.recip[:, g % 2], ctx[:, :, :, DK]).then_inc(self.s_recips, 1)
        dve.wait_ge(self.s_recips, b * NG + (g + 1))
        v.tensor_tensor(t.ctxn[:, :, HG * g:HG * (g + 1), :], ctx[:, :, :, 0:DK],
                        t.recip[:, g % 2].unsqueeze(3).to_broadcast([P, NT, HG, DK]),
                        ALU.mult).then_inc(self.s_dve_read, 1)

    def pe_cT(self, pe, b):
        bank = self.pe_bank(pe, b, ("cT",))
        pe.wait_ge(self.s_dve_read, self.plan.read(b, ("ctxT", NG - 1)))
        for i in range(NT):
            last = pe.transpose(bank[:, i * P:(i + 1) * P], self.t.ctxn[:, i].rearrange("p h d -> p (h d)"),
                                self.w.ident[:, :])
        last.then_inc(self.s_filled, 1)

    def act_cT(self, act, b):
        act.wait_ge(self.s_filled, self.plan.filled(b, ("cT",)))
        act.activation(self.t.cT[:, HI], self.bank(("cT",)), ACT.Copy).then_inc(self.s_cT_hi, 1)

    def dve_cT(self, dve, b):
        t, bank = self.t, self.bank(("cT",))
        dve.wait_ge(self.s_cT_hi, b + 1)
        self.nc.vector.tensor_tensor(t.cT[:, LO], bank, t.cT[:, HI].bitcast(F32), ALU.subtract)\
            .then_inc(self.s_dve_read, 1)

    def pe_wo(self, pe, b):
        t = self.t
        bank = self.pe_bank(pe, b, ("wo",))
        pe.wait_ge(self.s_dve_read, self.plan.read(b, ("cT",)))
        product(pe, bank, lambda k, p: t.wa[:, p, 3 * D:4 * D], lambda k, p: t.cT[:, p], 1,
                SPLIT3).then_inc(self.s_filled, 1)

    def act_wo(self, act, b):
        act.wait_ge(self.s_filled, self.plan.filled(b, ("wo",)))
        act.activation(self.t.aT[:, :], self.bank(("wo",)), ACT.Copy).then_inc(self.s_act_read, 1)

    def pe_attn(self, pe, b):
        bank = self.pe_bank(pe, b, ("attn",))
        pe.wait_ge(self.s_act_read, self.plan.read(b, ("wo",)))
        for i in range(NT):
            last = pe.transpose(bank[:, i * P:(i + 1) * P], self.t.aT[:, i * P:(i + 1) * P], self.w.ident[:, :])
        last.then_inc(self.s_filled, 1)

    def dve_attn(self, dve, b, s):
        dve.wait_ge(self.s_filled, self.plan.filled(b, ("attn",)))
        y2, xs = (v[:, s].rearrange("p i d -> p (i d)") for v in (self.y2, self.x))
        self.nc.vector.tensor_tensor(y2, y2, self.bank(("attn",)), ALU.add).then_inc(self.s_dve_read, 1)
        dve.wait_ge(self.s_dve_read, self.plan.read(b, ("attn",)))
        self.nc.vector.tensor_tensor(xs, xs, y2, ALU.add).then_inc(self.s_x_done, 1)


class FfnWeights:

    def __init__(self, nc, sb, sem, drams):
        self.nc = nc
        self.w1, self.w2 = sb("w1", [P, 2, HID], F32R), sb("w2", [P, 2, HID], F32R)
        self.h1, self.h2 = sb("h1", [P, 2, KC, HID], F32R), sb("h2", [P, 2, KC, HID], F32R)
        self.w3 = sb("w3", [P, 2, KC, D], F32R)
        raw12 = sb("raw12", [P, 2, HID], F32)
        rawh = [sb(f"rawh{n}", [P, KC, HID], F32) for n in range(2)]
        raw3 = sb("raw3", [P, KC, D], F32)
        w12, h, w3 = drams
        self.pieces = [(w12[0], raw12[:, 0], self.w1), (w12[1], raw12[:, 1], self.w2),
                       (h[0].rearrange("(k p) o -> p k o", p=P), rawh[0][:, :, :], self.h1),
                       (h[1].rearrange("(k p) o -> p k o", p=P), rawh[1][:, :, :], self.h2),
                       (w3.rearrange("(k p) o -> p k o", p=P), raw3[:, :, :], self.w3)]
        self.loaded = [sem(f"w_loaded{n}") for n in range(len(self.pieces))]
        self.hi_done, self.lo_done = sem("w_hi_done"), sem("w_lo_done")

    def sp_load(self, sp, which):
        for n in which:
            src, raw, _ = self.pieces[n]
            sp.dma_start(raw, src).then_inc(self.loaded[n], 16)

    def act_hi(self, act, which):
        for n in which:
            _, raw, split = self.pieces[n]
            act.wait_ge(self.loaded[n], 16)
            act.activation(split[:, HI], raw, ACT.Copy).then_inc(self.hi_done, 1)

    def dve_lo(self, dve, which):
        for n in which:
            _, raw, split = self.pieces[n]
            dve.wait_ge(self.hi_done, n + 1)
            self.nc.vector.tensor_tensor(split[:, LO], raw, split[:, HI].bitcast(F32),
                                         ALU.subtract).then_inc(self.lo_done, 1)


def bass_macaron(nc, x_in, ffn_w12, ffn_h, ffn_w3, ffn_scales, ffn_s3, attn_qkvo, attn_w13, attn_w2,
                 attn_norms, tables, out):
    half = B // 2
    with ExitStack() as ctx:
        def sem(name):
            return ctx.enter_context(nc.semaphore(name))

        def keep(name, shape, dt):
            return ctx.enter_context(nc.sbuf_tensor(name, shape, dt))

        class Constants:
            scale = keep("scale", [P, 4, KC], F32)
            half_s3 = keep("half_s3", [P, 1], F32)
            norms = keep("norms", [P, 2], F32)
            ident = keep("ident", [P, P], F32)
            minus_half = keep("minus_half", [P, NT], F32)
            eps = keep("eps", [P, NT], F32)

        w = Constants()
        ones = keep("ones", [P, 1], F32)
        lo_sums = keep("lo_sums", [P, 8], F32)
        flag = keep("flag", [1, 1], I32)
        x = keep("x", [P, B, NT, D], F32)
        y2 = keep("y2", [P, B, NT, D], F32)
        psum = ctx.enter_context(nc.psum_tensor("psum", [P, 8, S], F32))
        drams = (ffn_w12, ffn_h, ffn_w3)

        with ExitStack() as scope:
            def sb(name, shape, dt):
                return scope.enter_context(nc.sbuf_tensor("b1_" + name, shape, dt))

            def sem1(name):
                return sem("b1_" + name)

            plan = BankPlan(ffn_uses(), RING8)
            fw = FfnWeights(nc, sb, sem1, drams)
            f = Ffn(nc, sb, sem1, psum, w, fw, plan, inner=False)
            x_loaded = [sem(f"x_loaded{n}") for n in range(2)]
            const_loaded, const_set, w_sum = sem("const_loaded"), sem("const_set"), sem("w_sum")
            sums_added, flag_sum, flag_ready = sem("sums_added"), sem("flag_sum"), sem("flag_ready")
            pieces = list(range(5))

            def x_view(lo, hi):
                return x_in[lo:hi].rearrange("b (i p) d -> p b i d", p=P)

            with nc.Block() as block:
                @block.sync
                def _(sp):
                    fw.sp_load(sp, [0])
                    sp.dma_start(x[:, 0:2], x_view(0, 2)).then_inc(x_loaded[0], 16)
                    fw.sp_load(sp, pieces[1:])
                    sp.dma_start(w.ident[:, :], tables[:, 0:P]).then_inc(const_loaded, 16)
                    sp.dma_start(w.scale[:, :, :], ffn_scales).then_inc(const_loaded, 16)
                    sp.dma_start(w.half_s3[:, :], ffn_s3).then_inc(const_loaded, 16)
                    sp.dma_start(w.norms[:, :], attn_norms).then_inc(const_loaded, 16)
                    sp.dma_start(x[:, 2:B], x_view(2, B)).then_inc(x_loaded[1], 16)

                @block.gpsimd
                def _(pool):
                    pool.wait_ge(const_set, 1)
                    with pool.Fori(0, half) as it:
                        for j in range(2):
                            f.pool_rstd(pool, it, 0, j, mean_square=False)

                @block.scalar
                def _(act):
                    act.sem_inc(f.act_read, plan.per["act"])
                    fw.act_hi(act, pieces)
                    act.wait_ge(const_set, 1)
                    for n, (_, raw, split) in enumerate(fw.pieces):
                        act.wait_ge(fw.lo_done, n + 1)
                        act.activation(raw, split[:, LO].bitcast(F32), ACT.Abs,
                                       accum_out=lo_sums[:, n:n + 1]).then_inc(w_sum, 1)
                    act.wait_ge(const_set, 2)
                    with act.Fori(0, half) as it:
                        f.act_outer(act, it)

                @block.vector
                def _(dve):
                    dve.sem_inc(f.dve_read, plan.per["dve"])
                    dve.sem_inc(f.xT_read, 2)
                    nc.vector.memset(w.minus_half[:, :], -0.5)
                    nc.vector.memset(w.eps[:, :], EPS)
                    nc.vector.memset(lo_sums[:, :], 0.0)
                    nc.vector.memset(ones[:, :], 1.0).then_inc(const_set, 1)
                    dve.wait_ge(x_loaded[0], 16)
                    for j in range(2):
                        f.dve_moments(dve, j, x[:, j])
                    for j in range(2):
                        dve.wait_ge(f.stats_ready, j + 1)
                        f.dve_aggregate(dve, j)
                    fw.dve_lo(dve, pieces)
                    for j in range(2):
                        f.dve_normalise(dve, 0, 0, j, x[:, j], True)
                    dve.wait_ge(const_loaded, 64)
                    nc.vector.tensor_scalar(w.half_s3[:, :], w.half_s3[:, :], 0.5, None,
                                            ALU.mult).then_inc(const_set, 1)
                    dve.wait_ge(w_sum, len(pieces))
                    nc.vector.tensor_reduce(lo_sums[:, 7:8], lo_sums[:, 0:5], AX_X,
                                            ALU.add).then_inc(sums_added, 1)
                    dve.wait_ge(flag_sum, 1)
                    nc.vector.tensor_scalar(flag[:, :], psum[0:1, 0, 0:1], 0.0, None,
                                            ALU.not_equal).then_inc(flag_ready, 1)

                    for j in range(2):
                        f.dve_split_xT(dve, 0, 0, j, None)

                    def pair(it, following):
                        for j in range(2):
                            f.dve_first(dve, it, j, "a", "u", w.scale[:, 1], 0)
                        f.dve_outer_rest(dve, it, x, following, x, None, True)

                    dve.wait_ge(x_loaded[1], 16)
                    with dve.Fori(0, half - 1) as it:
                        pair(it, it + 1)
                    pair(half - 1, None)

                @block.tensor
                def _(pe):
                    pe.wait_ge(const_loaded, 64)
                    pe.wait_ge(sums_added, 1)
                    pe.matmul(psum[0:1, 0, 0:1], lo_sums[:, 7:8], ones[:, :], start=True,
                              stop=True).then_inc(flag_sum, 1)
                    pe.wait_ge(flag_ready, 1)
                    has_lo = pe.value_load(flag[0:1, 0:1])

                    def pair(it, following, parts):
                        for j in range(2):
                            f.pe_outer_first(pe, it, j, parts)
                        f.pe_outer_rest(pe, it, parts, following)

                    def loop(parts):
                        with pe.Fori(0, half - 1) as it:
                            pair(it, it + 1, parts)
                        pair(half - 1, None, parts)

                    for j in range(2):
                        f.pe_transpose_in(pe, 0, 0, j)
                    with pe.If(has_lo != 0):
                        loop(ALL4)
                    with pe.Else():
                        loop(EXACT_W)

        with ExitStack() as scope:
            def sb(name, shape, dt):
                return scope.enter_context(nc.sbuf_tensor("b2_" + name, shape, dt))

            bufs = AttentionBuffers(sb)
            raw = sb("raw", [P, 4 * D], F32)
            raw_mask = sb("raw_mask", [P, P], F32)
            shared = sem("ext_loaded"), sem("m_loaded")
            loads = EXT_DMAS * 16

            def attention(prefix, uses, first):
                return Attention(nc, bufs, psum, w, x, y2, BankPlan(uses, RING),
                                 lambda n: sem(prefix + n), shared, first)

            a = attention("b2a_", prologue_uses(), 0)
            wa_loaded, tab_loaded, wa_hi, wa_lo, set16 = (sem("wa_loaded"), sem("tab_loaded"), sem("wa_hi"),
                                                          sem("wa_lo"), sem("set16"))
            ones_loaded = sem("ones_loaded")
            with nc.Block() as block:
                @block.sync
                def _(sp):
                    sp.dma_start(raw[:, :], attn_qkvo).then_inc(wa_loaded, 16)
                    sp.dma_start(raw_mask[:, :], tables[:, P:2 * P]).then_inc(tab_loaded, 16)
                    sp.dma_start(bufs.tab[:, :, :, :].rearrange("p n i d -> p (n i d)"),
                                 tables[:, 2 * P:]).then_inc(tab_loaded, 16)
                    sp.wait_ge(set16, 2)
                    for par in range(2):
                        sp.dma_start(bufs.ext[par][1][M_ROW:M_ROW + 2, :, :],
                                     bufs.fill16[:, 1, :]).then_inc(ones_loaded, 16)
                    a.sp_ext(sp, 0, 0)
                    sp.wait_ge(shared[1], 64)

                @block.gpsimd
                def _(pool):
                    a.pool_factors(pool, 0)
                    a.pool_parts(pool, 0)
                    a.pool_factors(pool, 1)

                @block.scalar
                def _(act):
                    act.sem_inc(a.s_act_read, a.plan.per["act"])
                    act.wait_ge(wa_loaded, 16)
                    act.activation(bufs.wa[:, HI], raw[:, :], ACT.Copy).then_inc(wa_hi, 1)
                    a.act_hT(act, 0)
                    a.act_qkT(act, 0, None)
                    for n in range(2):
                        a.act_parts(act, 0, n)
                    a.act_mT(act, 0, 0, None, 0)
                    a.act_mT(act, 0, 1, 32, 0)

                @block.vector
                def _(dve):
                    v = nc.vector
                    dve.sem_inc(a.s_dve_read, a.plan.per["dve"])
                    a.dve_moments(dve, 0, 0)
                    dve.wait_ge(a.s_stats_ready, 1)
                    a.dve_aggregate(dve, 0)
                    v.memset(bufs.zero[:, :], 0.0)
                    v.memset(bufs.fill16[:, 0, :], 0.0)
                    v.memset(bufs.fill16[:, 1, :], 1.0)
                    for par in range(2):
                        for n in range(2):
                            v.memset(bufs.ext[par][n][64:NE, :, :], 0.0)
                        v.memset(bufs.V[par][:, :, :, :], 0.0)
                    v.memset(psum[:, CTX_BANK, :], 0.0)
                    v.tensor_copy(bufs.ident16[:, :], w.ident[:, :]).then_inc(set16, 1)
                    dve.wait_ge(set16, 1)
                    for par in range(2):
                        last = v.memset(bufs.V[par][:, :, :, DK:DK + 1], 1.0)
                    last.then_inc(set16, 1)
                    a.dve_normalise(dve, 0, 0)
                    a.dve_layernorm(dve, 0, 0)
                    a.dve_moments(dve, 1, 1)
                    dve.wait_ge(wa_hi, 1)
                    v.tensor_tensor(bufs.wa[:, LO], raw[:, :], bufs.wa[:, HI].bitcast(F32),
                                    ALU.subtract).then_inc(wa_lo, 1)
                    dve.wait_ge(tab_loaded, 32)
                    v.tensor_copy(bufs.mask16[:, :], raw_mask[:, :]).then_inc(set16, 1)
                    a.dve_hT(dve, 0)
                    dve.wait_ge(set16, 3)
                    a.dve_rope(dve, 0, 0)
                    dve.wait_ge(a.s_stats_ready, 2)
                    a.dve_rest(dve, 0)
                    a.dve_aggregate(dve, 1)
                    for g in range(2):
                        a.dve_max(dve, 0, g)
                        a.dve_max_parts(dve, 0, g, g)

                @block.tensor
                def _(pe):
                    a.pe_hT(pe, 0)
                    pe.wait_ge(wa_lo, 1)
                    for i in range(NT):
                        a.pe_qkv(pe, 0, i)
                    a.pe_qkT(pe, 0)
                    pe.wait_ge(ones_loaded, 32)
                    pe.wait_ge(set16, 3)
                    a.pe_max(pe, 0, 0, 0, loads)
                    a.pe_mT(pe, 0, 0, 0)
                    a.pe_max(pe, 0, 1, 0, None)
                    a.pe_mT(pe, 0, 1, 1)

            a2 = attention("b2b_", attention_uses(last=False), 0)
            a3 = attention("b2c_", attention_uses(last=True), B - 1)

            def pool_body(pool, a, b, last, stats):
                a.pool_mask(pool, b, 0)
                if not last:
                    a.pool_parts(pool, b)
                a.pool_mask(pool, b, 1)
                if stats:
                    a.pool_factors(pool, b)
                a.pool_mask(pool, b, 2)
                a.pool_mask(pool, b, 3)

            def act_body(act, a, b, par, last):
                seq = b + a.first
                a.act_exp(act, b, 0, range(0, 2))
                if not last:
                    a.act_hT(act, b)
                a.act_exp(act, b, 0, range(2, UNITS))
                a.act_context(act, b, 0)
                if not last:
                    a.act_qkT(act, b, seq * loads + loads)
                for n in range(2):
                    a.act_exp(act, b, 1, [n])
                    if not last:
                        a.act_parts(act, b, n)
                a.act_exp(act, b, 1, range(2, UNITS))
                a.act_mT(act, b, 2, seq * (NG * 32) + 64, par)
                a.act_context(act, b, 1)
                a.act_exp(act, b, 2)
                a.act_mT(act, b, 3, seq * (NG * 32) + 96, par)
                a.act_context(act, b, 2)
                a.act_exp(act, b, 3)
                if not last:
                    a.act_mT(act, b, 0, seq * (NG * 32) + 128, 1 - par)
                a.act_context(act, b, 3)
                a.act_cT(act, b)
                a.act_wo(act, b)
                if not last:
                    a.act_mT(act, b, 1, seq * (NG * 32) + 160, 1 - par)

            def dve_body(dve, a, b, par, last, stats):
                nxt, s = 1 - par, b + a.first
                if not last:
                    a.dve_normalise(dve, b, s + 1)
                    a.dve_layernorm(dve, b, s + 1)
                    a.dve_hT(dve, b)
                    a.dve_rope(dve, b, nxt)
                if stats:
                    a.dve_moments(dve, b, s + 2)
                    dve.wait_ge(a.s_stats_ready, b + 1)
                if not last:
                    a.dve_rest(dve, b)
                if stats:
                    a.dve_aggregate(dve, b)
                a.dve_max(dve, b, 2)
                a.dve_max_parts(dve, b, 2, 0)
                a.dve_max(dve, b, 3, cut_units(3, CUTS, 0, 3))
                a.dve_ctxT(dve, b, 0)
                a.dve_max(dve, b, 3, cut_units(3, CUTS, 3, 4))
                a.dve_max_parts(dve, b, 3, 1)
                if not last:
                    a.dve_max(dve, b, 0, cut_units(0, CUTS, 0, 3))
                a.dve_ctxT(dve, b, 1)
                if not last:
                    a.dve_max(dve, b, 0, cut_units(0, CUTS, 3, 4))
                    a.dve_max_parts(dve, b, 0, 2)
                    a.dve_max(dve, b, 1, cut_units(1, TAIL, 0, 3))
                a.dve_ctxT(dve, b, 2)
                if not last:
                    a.dve_max(dve, b, 1, cut_units(1, TAIL, 3, 4))
                a.dve_ctxT(dve, b, 3)
                if not last:
                    a.dve_max(dve, b, 1, cut_units(1, TAIL, 4, 5))
                a.dve_cT(dve, b)
                if not last:
                    a.dve_max(dve, b, 1, cut_units(1, TAIL, 5, 6))
                    a.dve_max_parts(dve, b, 1, 3)
                a.dve_attn(dve, b, s)

            def beside(pe, a, b, g, par, max_group, max_par, units, first=0):
                left = len(units)
                for u in range(first, UNITS):
                    part = -(-left // (UNITS - u))
                    a.pe_scores(pe, b, g, par, [u])
                    if part:
                        a.pe_max(pe, b, max_group, max_par, None, units[len(units) - left:len(units) - left + part])
                    left -= part

            def context(pe, a, b, g, par, max_group, max_par, units):
                for j in range(NT):
                    a.pe_context(pe, b, g, par, j)
                    a.pe_max(pe, b, max_group, max_par, None, units[j:j + 1])

            def pe_body(pe, a, b, par, last):
                nxt, seq = 1 - par, b + a.first
                a.pe_scores(pe, b, 0, par, range(0, 2))
                if not last:
                    a.pe_hT(pe, b)
                a.pe_scores(pe, b, 0, par, range(2, UNITS))
                if not last:
                    for i in range(NT):
                        a.pe_qkv(pe, b, i)
                context(pe, a, b, 0, par, 2, par, [])
                if not last:
                    a.pe_qkT(pe, b)
                beside(pe, a, b, 1, par, 2, par, max_units(2), 0)
                a.pe_max(pe, b, 3, par, None, cut_units(3, CUTS, 0, 1))
                a.pe_mT(pe, b, 2, 0)
                a.pe_max(pe, b, 3, par, None, cut_units(3, CUTS, 1, 2))
                context(pe, a, b, 1, par, 3, par, cut_units(3, CUTS, 2, 3))
                a.pe_ctxT(pe, b, 0)
                beside(pe, a, b, 2, par, 3, par, cut_units(3, CUTS, 3, 4))
                if not last:
                    a.pe_max(pe, b, 0, nxt, seq * loads + 2 * loads, cut_units(0, CUTS, 0, 1))
                a.pe_mT(pe, b, 3, 1)
                if not last:
                    a.pe_max(pe, b, 0, nxt, None, cut_units(0, CUTS, 1, 2))
                context(pe, a, b, 2, par, 0, nxt, [] if last else cut_units(0, CUTS, 2, 3))
                a.pe_ctxT(pe, b, 1)
                beside(pe, a, b, 3, par, 0, nxt, [] if last else cut_units(0, CUTS, 3, 4))
                if not last:
                    a.pe_max(pe, b, 1, nxt, None, cut_units(1, TAIL, 0, 1))
                    a.pe_mT(pe, b, 0, 2)
                    a.pe_max(pe, b, 1, nxt, None, cut_units(1, TAIL, 1, 2))
                context(pe, a, b, 3, par, 1, nxt, [] if last else cut_units(1, TAIL, 2, 3))
                a.pe_ctxT(pe, b, 2)
                if not last:
                    a.pe_max(pe, b, 1, nxt, None, cut_units(1, TAIL, 3, 4))
                a.pe_ctxT(pe, b, 3)
                if not last:
                    a.pe_max(pe, b, 1, nxt, None, cut_units(1, TAIL, 4, 5))
                a.pe_cT(pe, b)
                if not last:
                    a.pe_max(pe, b, 1, nxt, None, cut_units(1, TAIL, 5, 6))
                a.pe_wo(pe, b)
                if not last:
                    a.pe_mT(pe, b, 1, 3)
                a.pe_attn(pe, b)

            def attention_block(a, n, last):
                def all_sequences(eng, body):
                    if n > 1:
                        with eng.Fori(0, n // 2) as pair:
                            for par in range(2):
                                body(pair * 2 + par, par, True)
                    if n % 2:
                        body(n - 1, (a.first + n - 1) % 2, False)

                with nc.Block() as block:
                    @block.sync
                    def _(sp):
                        if not last:
                            all_sequences(sp, lambda b, par, _: a.sp_ext(sp, b, 1 - par))
                        sp.wait_ge(shared[1], (a.first + n) * NG * 32 + (0 if last else 64))

                    @block.gpsimd
                    def _(pool):
                        pool.sem_inc(a.s_masks, 1)
                        pool.sem_inc(a.s_factors, 1)
                        all_sequences(pool, lambda b, par, stats: pool_body(pool, a, b, last, stats))

                    @block.scalar
                    def _(act):
                        act.sem_inc(a.s_act_read, a.plan.per["act"])
                        act.sem_inc(a.s_exps, 2)
                        act.sem_inc(a.s_ctx_read, 1)
                        all_sequences(act, lambda b, par, _: act_body(act, a, b, par, last))

                    @block.vector
                    def _(dve):
                        dve.sem_inc(a.s_dve_read, a.plan.per["dve"])
                        all_sequences(dve, lambda b, par, stats: dve_body(dve, a, b, par, last, stats))

                    @block.tensor
                    def _(pe):
                        pe.sem_inc(a.s_ctx, NG)
                        all_sequences(pe, lambda b, par, _: pe_body(pe, a, b, par, last))

            attention_block(a2, B - 1, last=False)
            attention_block(a3, 1, last=True)

        with ExitStack() as scope:
            def sb(name, shape, dt):
                return scope.enter_context(nc.sbuf_tensor("b3_" + name, shape, dt))

            def sem3(name):
                return sem("b3_" + name)

            plan = BankPlan(inner_ffn_uses() + ffn_uses(), RING8)
            fw = FfnWeights(nc, sb, sem3, drams)
            f = Ffn(nc, sb, sem3, psum, w, fw, plan, inner=True)
            iw = [sb(f"iw{n}", [P, 2, HID], F32R) for n in range(3)]
            raw = [f.g[:, n] for n in range(3)]
            i_loaded = [sem3(f"i_loaded{n}") for n in range(3)]
            i_hi, i_lo, stored = sem3("i_hi"), sem3("i_lo"), sem3("stored")
            w2i = iw[2][:, :, :].rearrange("p n (k o) -> p n k o", k=KC)
            pieces = list(range(5))
            out_pairs = out.rearrange("(n j) (i p) d -> n p j i d", j=2, p=P)
            x_pairs = x[:, :, :, :].rearrange("p (n j) i d -> p n j i d", j=2)

            with nc.Block() as block:
                @block.sync
                def _(sp):
                    for n in range(2):
                        sp.dma_start(raw[n], attn_w13[n]).then_inc(i_loaded[n], 16)
                    sp.dma_start(raw[2].rearrange("p (k o) -> p k o", k=KC),
                                 attn_w2.rearrange("(k p) o -> p k o", p=P)).then_inc(i_loaded[2], 16)
                    fw.sp_load(sp, pieces)
                    with sp.Fori(0, half) as it:
                        sp.wait_ge(f.dve_read, plan.read(it, ("yT", 1)))
                        sp.dma_start(out_pairs[it], x_pairs[:, it]).then_inc(stored, 16)
                    sp.wait_ge(stored, 16 * half)

                @block.gpsimd
                def _(pool):
                    for j in range(2):
                        f.pool_rstd(pool, 0, 0, j, mean_square=True)
                    with pool.Fori(0, half - 1) as it:
                        for j in range(2):
                            f.pool_rstd(pool, it, 1, j, mean_square=False)
                        for j in range(2):
                            f.pool_rstd(pool, it + 1, 0, j, mean_square=True)
                    for j in range(2):
                        f.pool_rstd(pool, half - 1, 1, j, mean_square=False)

                @block.scalar
                def _(act):
                    act.sem_inc(f.act_read, plan.per["act"])
                    for n in range(3):
                        act.wait_ge(i_loaded[n], 16)
                        act.activation(iw[n][:, HI], raw[n], ACT.Copy).then_inc(i_hi, 1)
                    fw.act_hi(act, pieces)
                    with act.Fori(0, half) as it:
                        f.act_first(act, it, 0, "ia", None, 0)
                        f.act_first(act, it, 1, "ia", None, 0, range(0, 2))
                        f.act_out(act, it, 0, "iy", None)
                        f.act_first(act, it, 1, "ia", None, 0, range(2, KC + 1))
                        f.act_out(act, it, 1, "iy", None)
                        f.act_outer(act, it)

                @block.vector
                def _(dve):
                    dve.sem_inc(f.dve_read, plan.per["dve"])
                    dve.sem_inc(f.xT_read, 2)

                    def split_weights():
                        for n in range(3):
                            dve.wait_ge(i_hi, n + 1)
                            nc.vector.tensor_tensor(iw[n][:, LO], raw[n], iw[n][:, HI].bitcast(F32),
                                                    ALU.subtract).then_inc(i_lo, 1)

                    def aggregate(it, which, j):
                        dve.wait_ge(f.stats_ready, f.norm_count(it, which, j))
                        nc.vector.memset(f.spare[:, j:j + 1], 0.0)
                        f.dve_aggregate(dve, j)

                    def flat(v):
                        return v.rearrange("p i d -> p (i d)")

                    def pair(it, following):
                        def first(j, steps):
                            f.dve_first(dve, it, j, "ia", "iu", None, 0, steps)

                        def add(j):
                            f.dve_add(dve, it, j, "iyT", flat(x[:, it * 2 + j]))

                        def moments(j):
                            dve.wait_ge(f.dve_read, plan.read(it, ("iyT", j)))
                            nc.vector.memset(f.spare[:, 2 + j:3 + j], 0.0)
                            f.dve_moments(dve, j, x[:, it * 2 + j])

                        first(0, range(KC + 1))
                        first(1, range(0, 3))
                        add(0)
                        first(1, [3])
                        moments(0)
                        first(1, [4])
                        aggregate(it, 1, 0)
                        f.dve_normalise(dve, it, 1, 0, x[:, it * 2], True)
                        add(1)
                        moments(1)
                        aggregate(it, 1, 1)
                        f.dve_split_xT(dve, it, 1, 0, None)
                        f.dve_normalise(dve, it, 1, 1, x[:, it * 2 + 1], True)
                        f.dve_first(dve, it, 0, "a", "u", w.scale[:, 1], 0, range(KC))
                        f.dve_split_xT(dve, it, 1, 1, None)
                        f.dve_first(dve, it, 0, "a", "u", w.scale[:, 1], 0, [KC])
                        f.dve_first(dve, it, 1, "a", "u", w.scale[:, 1], 0)
                        f.dve_outer_rest(dve, it, x, following, y2, w.norms[:, 1:2], False)

                    for j in range(2):
                        f.dve_moments(dve, j, y2[:, j])
                    for j in range(2):
                        aggregate(0, 0, j)
                    split_weights()
                    for j in range(2):
                        f.dve_normalise(dve, 0, 0, j, y2[:, j], False)
                    for j in range(2):
                        f.dve_split_xT(dve, 0, 0, j, w.norms[:, 1:2])
                    fw.dve_lo(dve, pieces)
                    with dve.Fori(0, half - 1) as it:
                        pair(it, it + 1)
                    pair(half - 1, None)

                @block.tensor
                def _(pe):
                    def pair(it, following, parts):
                        def first(j, chunks):
                            f.pe_first(pe, it, 0, j, ("ia", "iu"), (iw[0], iw[1]), SPLIT3, chunks)

                        first(0, range(KC))
                        first(1, range(2))
                        f.pe_out(pe, it, 0, "iy", "ia", w2i, 0, SPLIT3)
                        first(1, [2])
                        f.pe_transpose_out(pe, it, 0, "iyT", "iy")
                        first(1, [3])
                        f.pe_out(pe, it, 1, "iy", "ia", w2i, 0, SPLIT3)
                        f.pe_transpose_out(pe, it, 1, "iyT", "iy")
                        f.pe_transpose_in(pe, it, 1, 0)
                        pe.wait_ge(fw.lo_done, len(pieces))
                        f.pe_outer_first(pe, it, 0, parts)
                        f.pe_transpose_in(pe, it, 1, 1)
                        f.pe_outer_first(pe, it, 1, parts)
                        f.pe_outer_rest(pe, it, parts, following)

                    def loop(parts):
                        with pe.Fori(0, half - 1) as it:
                            pair(it, it + 1, parts)
                        pair(half - 1, None, parts)

                    has_lo = pe.value_load(flag[0:1, 0:1])
                    for j in range(2):
                        f.pe_transpose_in(pe, 0, 0, j)
                    pe.wait_ge(i_lo, 3)
                    with pe.If(has_lo != 0):
                        loop(ALL4)
                    with pe.Else():
                        loop(EXACT_W)


def kernel(**inputs):
    import numpy as np
    import concourse.bacc as bacc
    from concourse.bass_utils import run_bass_kernel_spmd

    a = {k.removeprefix("L0_"): np.asarray(v) for k, v in inputs.items()}
    pos = np.arange(S, dtype=np.float32)
    k = (np.arange(DK) // 2).astype(np.float32)
    angles = pos[:, None] / np.power(np.float32(10000.0), np.float32(2.0) * k / np.float32(DK))
    sign = np.where(np.arange(DK) % 2 == 0, 1.0, -1.0).astype(np.float32)
    cos, sin = np.cos(angles), np.sin(angles) * sign

    def tiles(t):
        return t.reshape(NT, P, DK).transpose(1, 0, 2).reshape(P, NT * DK)

    mask = np.where(np.arange(P)[None, :] > np.arange(P)[:, None], MASKED, 0.0)
    tables = np.concatenate([np.eye(P), mask, tiles(cos), tiles(sin)], axis=1).astype(np.float32)
    arrays = {
        "x": a["attn_x"],
        "ffn_w12": np.stack([a["ffn_w1_w"].T, a["ffn_w2_w"].T]),
        "ffn_h": np.stack([a["ffn_h1_w"].T, a["ffn_h2_w"].T]),
        "ffn_w3": a["ffn_w3_w"].T,
        "ffn_scales": np.stack([a[f"ffn_{n}_s"].reshape(KC, P).T for n in ("w1", "w2", "h1", "h2")], axis=1),
        "ffn_s3": a["ffn_w3_s"].reshape(P, 1),
        "attn_qkvo": np.concatenate([a[f"attn_{n}"].T for n in ("wq", "wk", "wv", "wo")], axis=1),
        "attn_w13": np.stack([a["attn_w1"].T, a["attn_w3"].T]),
        "attn_w2": a["attn_w2"].T,
        "attn_norms": np.stack([a["attn_norm1_w"], a["attn_norm2_w"]], axis=1),
        "tables": tables,
    }
    nc = bacc.Bacc("TRN2", target_bir_lowering=False, num_devices=1)
    fed, args = {}, []
    for name, v in arrays.items():
        v = np.ascontiguousarray(v)
        fed[f"in_{name}"] = v
        args.append(nc.dram_tensor(f"in_{name}", v.shape, mybir.dt.from_np(v.dtype), kind="ExternalInput").ap())
    out = nc.dram_tensor("out_x", (B, S, D), F32, kind="ExternalOutput").ap()
    bass_macaron(nc, *args, out)
    r = run_bass_kernel_spmd(nc, [fed], core_ids=[0])
    return r.results[0]["out_x"]
```

```python
from contextlib import ExitStack

import concourse.bass as bass
from concourse import mybir

F32 = mybir.dt.float32
F32R = mybir.dt.float32r
BF16 = mybir.dt.bfloat16
I32 = mybir.dt.int32
ALU = mybir.AluOpType
ACT = mybir.ActivationFunctionType
AX_X = mybir.AxisListType.X

P = 128
B, S, D = 8, 512, 128
NT = S // P
HID = 512
KC = HID // P
NH, DK = 16, 8
HG = 4
NG = NH // HG
EPS = 1e-5
SCALE = DK ** -0.5
MASKED = -1e30
HI, LO = 0, 1

EXACT_W = [(HI, HI), (HI, LO)]
ALL4 = [(HI, HI), (LO, HI), (LO, LO), (HI, LO)]
SPLIT3 = [(HI, HI), (LO, HI), (HI, LO)]

NE = 96
NPART = 3
M_ROW = NPART * NPART * DK


class BankPlan:

    def __init__(self, uses, banks):
        self.uses, self.banks, self.n = uses, banks, len(uses)
        self.index = {name: i for i, (name, _) in enumerate(uses)}
        assert len(self.index) == self.n
        self.per = {e: sum(r == e for _, r in uses) for e in ("act", "dve")}

    def bank(self, name):
        return self.banks[self.index[name] % len(self.banks)]

    def filled(self, it, name):
        return it * self.n + (self.index[name] + 1)

    def read(self, it, name):
        i = self.index[name]
        who = self.uses[i][1]
        return it * self.per[who] + (self.per[who] + sum(r == who for _, r in self.uses[:i + 1]))

    def last_user(self, it, name):
        i = self.index[name] % len(self.banks)
        before = [k for k in range(self.index[name]) if k % len(self.banks) == i]
        if before:
            k = before[-1]
            return self.uses[k][1], self.read(it, self.uses[k][0])
        k = [k for k in range(self.n) if k % len(self.banks) == i][-1]
        who = self.uses[k][1]
        return who, it * self.per[who] + sum(r == who for _, r in self.uses[:k + 1])


def ffn_uses():
    uses = []
    for j in range(2):
        for c in range(KC):
            uses += [(("a", j, c), "act"), (("u", j, c), "dve")]
    for layer in ("h1", "h2"):
        uses += [((layer, j, c), "act") for j in range(2) for c in range(KC)]
    uses += [(("y", j), "act") for j in range(2)]
    uses += [(("yT", j), "dve") for j in range(2)]
    return uses


def inner_ffn_uses():
    def first(j, chunks):
        return [use for c in chunks for use in ((("ia", j, c), "act"), (("iu", j, c), "dve"))]

    return (first(0, range(KC)) + first(1, range(2)) + [(("iy", 0), "act")] + first(1, [2])
            + [(("iyT", 0), "dve")] + first(1, [3]) + [(("iy", 1), "act"), (("iyT", 1), "dve")])


FFN_RING = list(range(6))
T_BANK = 6


def product(pe, out, weights, data, chunks, parts):
    order = [(k, w, d) for k in range(chunks) for w, d in parts]
    for n, (k, w, d) in enumerate(order):
        last = pe.matmul(out, weights(k, w), data(k, d), start=(n == 0), stop=(n == len(order) - 1))
    return last


class Ffn:

    NSLOT = 4

    def __init__(self, nc, sb, sem, psum, constants, weights, plan, inner):
        self.nc, self.psum, self.plan = nc, psum, plan
        self.w, self.fw = constants, weights
        self.xn = sb("xn", [P, 2, NT, D], F32)
        self.xT = sb("xT", [P, 2, 2, S], F32R)
        self.g = sb("g", [P, self.NSLOT, S], F32)
        self.hf = sb("hf", [P, self.NSLOT, S], F32)
        self.H = sb("H", [P, 2, 2, KC, 2, S], F32R)
        self.yT = sb("yT", [P, 2, S], F32)
        self.stats = sb("stats", [P, 2, NT, 6], F32)
        self.mv = sb("mv", [P, 2, NT, 2], F32)
        self.var = sb("var", [P, 2, NT], F32)
        self.rstd = sb("rstd", [P, 2, NT], F32)
        self.spare = sb("spare", [P, 4], F32)
        self.filled = sem("banks_filled")
        self.act_read, self.dve_read = sem("act_read"), sem("dve_read")
        self.hi_ready, self.lo_ready = sem("hi_ready"), sem("lo_ready")
        self.xn_ready, self.xT_hi = sem("xn_ready"), sem("xT_hi")
        self.xT_filled, self.xT_read = sem("xT_filled"), sem("xT_read")
        self.stats_ready, self.moments = sem("stats_ready"), sem("moments")
        self.pool_step, self.rstd_ready = sem("pool_step"), sem("rstd_ready")
        self.first = 2 * KC if inner else 0
        self.per = self.first + 6 * KC
        self.norms = 2 if inner else 1

    def read_sem(self, who):
        return self.act_read if who == "act" else self.dve_read

    def slot(self, layer, j, c):
        base = {"ia": 0, "a": self.first, "h1": self.first + 2 * KC, "h2": self.first + 4 * KC}[layer]
        return base + KC * j + c

    def bank(self, name):
        return self.psum[:, self.plan.bank(name), :]

    def norm_count(self, it, which, j):
        return (it * self.norms + which) * 2 + (j + 1)

    def pool_rstd(self, pool, it, which, j, mean_square):
        n = self.norm_count(it, which, j)
        pool.wait_ge(self.moments, n)
        steps = (n - 1) * 3
        if mean_square:
            self.nc.gpsimd.tensor_tensor(self.rstd[:, j], self.mv[:, j, :, 0], self.mv[:, j, :, 0],
                                         ALU.mult).then_inc(self.pool_step, 1)
            pool.wait_ge(self.pool_step, steps + 1)
            self.nc.gpsimd.tensor_tensor(self.var[:, j], self.mv[:, j, :, 1], self.rstd[:, j],
                                         ALU.add).then_inc(self.pool_step, 1)
            pool.wait_ge(self.pool_step, steps + 2)
            self.nc.gpsimd.tensor_tensor(self.var[:, j], self.var[:, j], self.w.eps[:, :],
                                         ALU.add).then_inc(self.pool_step, 1)
        else:
            self.nc.gpsimd.tensor_tensor(self.var[:, j], self.mv[:, j, :, 1], self.w.eps[:, :],
                                         ALU.add).then_inc(self.pool_step, 3)
        pool.wait_ge(self.pool_step, steps + 3)
        self.nc.gpsimd.tensor_tensor(self.rstd[:, j], self.var[:, j], self.w.minus_half[:, 0:NT],
                                     ALU.pow).then_inc(self.rstd_ready, 1)

    def dve_moments(self, dve, j, src):
        for i in range(NT):
            last = self.nc.vector.bn_stats(self.stats[:, j, i], src[:, i, :])
        last.then_inc(self.stats_ready, 1)

    def dve_aggregate(self, dve, j):
        for i in range(NT):
            last = self.nc.vector.bn_aggr(self.mv[:, j, i], self.stats[:, j, i])
        last.then_inc(self.moments, 1)

    def dve_normalise(self, dve, it, which, j, src, subtract_mean):
        n = self.norm_count(it, which, j)
        dve.wait_ge(self.rstd_ready, n)
        for i in range(NT):
            if subtract_mean:
                last = self.nc.vector.tensor_scalar(self.xn[:, j, i], src[:, i, :], self.mv[:, j, i, 0:1],
                                                    self.rstd[:, j, i:i + 1], ALU.subtract, ALU.mult)
            else:
                last = self.nc.vector.tensor_scalar(self.xn[:, j, i], src[:, i, :],
                                                    self.rstd[:, j, i:i + 1], None, ALU.mult)
        last.then_inc(self.xn_ready, 1)

    def act_xT(self, act, it, which, j, weight):
        n = self.norm_count(it, which, j)
        act.wait_ge(self.xT_filled, n)
        kw = {} if weight is None else {"scale": weight}
        act.activation(self.xT[:, j, HI], self.psum[:, T_BANK + j, :], ACT.Copy, **kw).then_inc(self.xT_hi, 1)

    def dve_xT(self, dve, it, which, j, weight):
        n = self.norm_count(it, which, j)
        bank, hi = self.psum[:, T_BANK + j, :], self.xT[:, j, HI].bitcast(F32)
        dve.wait_ge(self.xT_hi, n)
        if weight is None:
            last = self.nc.vector.tensor_tensor(self.xT[:, j, LO], bank, hi, ALU.subtract)
        else:
            last = self.nc.vector.scalar_tensor_tensor(self.xT[:, j, LO], bank, weight, hi, ALU.mult, ALU.subtract)
        last.then_inc(self.xT_read, 1)

    def pe_bank(self, pe, it, name):
        who, value = self.plan.last_user(it, name)
        pe.wait_ge(self.read_sem(who), value)
        return self.bank(name)

    def pe_transpose_in(self, pe, it, which, j):
        n = self.norm_count(it, which, j)
        bank = self.psum[:, T_BANK + j, :]
        pe.wait_ge(self.xT_read, n)
        pe.wait_ge(self.xn_ready, n)
        for i in range(NT):
            last = pe.transpose(bank[:, i * P:(i + 1) * P], self.xn[:, j, i, :], self.w.ident[:, :])
        last.then_inc(self.xT_filled, 1)

    def pe_first(self, pe, it, which, j, names, weights, parts, chunks=range(KC)):
        pe.wait_ge(self.xT_read, self.norm_count(it, which, j) + 2)
        for c in chunks:
            for name, w in zip(names, weights):
                bank = self.pe_bank(pe, it, (name, j, c))
                product(pe, bank, lambda k, p: w[:, p, c * P:(c + 1) * P],
                        lambda k, p: self.xT[:, j, p], 1, parts).then_inc(self.filled, 1)

    def pe_hidden(self, pe, it, j, layer, before, w, src, parts):
        for c in range(KC):
            bank = self.pe_bank(pe, it, (layer, j, c))
            order = [(k, wp, dp) for k in range(KC) for wp, dp in parts]
            for n, (k, wp, dp) in enumerate(order):
                if c == 0 and n % len(parts) == 0:
                    pe.wait_ge(self.lo_ready, it * self.per + self.slot(before, j, k) + 1)
                last = pe.matmul(bank, w[:, wp, k, c * P:(c + 1) * P], self.H[:, j, src, k, dp],
                                 start=(n == 0), stop=(n == len(order) - 1))
            last.then_inc(self.filled, 1)

    def pe_out(self, pe, it, j, name, before, w, src, parts):
        bank = self.pe_bank(pe, it, (name, j))
        order = [(k, wp, dp) for k in range(KC) for wp, dp in parts]
        for n, (k, wp, dp) in enumerate(order):
            if n % len(parts) == 0:
                pe.wait_ge(self.lo_ready, it * self.per + self.slot(before, j, k) + 1)
            last = pe.matmul(bank, w[:, wp, k, :], self.H[:, j, src, k, dp],
                             start=(n == 0), stop=(n == len(order) - 1))
        last.then_inc(self.filled, 1)

    def pe_transpose_out(self, pe, it, j, name, yname):
        bank = self.pe_bank(pe, it, (name, j))
        pe.wait_ge(self.act_read, self.plan.read(it, (yname, j)))
        for i in range(NT):
            last = pe.transpose(bank[:, i * P:(i + 1) * P], self.yT[:, j, i * P:(i + 1) * P], self.w.ident[:, :])
        last.then_inc(self.filled, 1)

    def act_slot_free(self, act, it, idx):
        if idx >= self.NSLOT:
            act.wait_ge(self.lo_ready, it * self.per + (idx - self.NSLOT + 1))

    def act_first(self, act, it, j, aname, scale, dst, steps=range(KC + 1)):
        for c in steps:
            if c < KC:
                idx = self.slot(aname, j, c)
                self.act_slot_free(act, it, idx)
                act.wait_ge(self.filled, self.plan.filled(it, (aname, j, c)))
                kw = {} if scale is None else {"scale": scale[:, c:c + 1]}
                act.activation(self.g[:, idx % self.NSLOT], self.bank((aname, j, c)), ACT.Silu,
                               **kw).then_inc(self.act_read, 1)
            if c > 0:
                idx = self.slot(aname, j, c - 1)
                uname = "iu" if aname == "ia" else "u"
                act.wait_ge(self.dve_read, self.plan.read(it, (uname, j, c - 1)))
                act.activation(self.H[:, j, dst, c - 1, HI], self.hf[:, idx % self.NSLOT],
                               ACT.Copy).then_inc(self.hi_ready, 1)

    def act_hidden(self, act, it, j, layer, scale, dst):
        for c in range(KC):
            idx = self.slot(layer, j, c)
            act.wait_ge(self.filled, self.plan.filled(it, (layer, j, c)))
            act.activation(self.H[:, j, dst, c, HI], self.bank((layer, j, c)), ACT.Gelu,
                           scale=scale[:, c:c + 1]).then_inc(self.hi_ready, 1)
            self.act_slot_free(act, it, idx)
            act.activation(self.g[:, idx % self.NSLOT], self.bank((layer, j, c)), ACT.Gelu,
                           scale=scale[:, c:c + 1]).then_inc(self.act_read, 1)

    def act_out(self, act, it, j, name, scale):
        act.wait_ge(self.filled, self.plan.filled(it, (name, j)))
        kw = {} if scale is None else {"scale": scale}
        act.activation(self.yT[:, j], self.bank((name, j)), ACT.Copy, **kw).then_inc(self.act_read, 1)

    def dve_first(self, dve, it, j, aname, uname, scale, dst, steps=range(KC + 1)):
        for c in steps:
            if c < KC:
                idx = self.slot(aname, j, c)
                if idx >= self.NSLOT:
                    dve.wait_ge(self.lo_ready, it * self.per + idx - self.NSLOT + 1)
                dve.wait_ge(self.act_read, self.plan.read(it, (aname, j, c)))
                dve.wait_ge(self.filled, self.plan.filled(it, (uname, j, c)))
                slot = idx % self.NSLOT
                s = 1.0 if scale is None else scale[:, c:c + 1]
                self.nc.vector.scalar_tensor_tensor(self.hf[:, slot], self.bank((uname, j, c)), s, self.g[:, slot],
                                                    ALU.mult, ALU.mult).then_inc(self.dve_read, 1)
            if c > 0:
                idx = self.slot(aname, j, c - 1)
                dve.wait_ge(self.hi_ready, it * self.per + idx + 1)
                self.nc.vector.tensor_tensor(self.H[:, j, dst, c - 1, LO], self.hf[:, idx % self.NSLOT],
                                             self.H[:, j, dst, c - 1, HI].bitcast(F32),
                                             ALU.subtract).then_inc(self.lo_ready, 1)

    def dve_hidden(self, dve, it, j, layer, dst):
        for c in range(KC):
            idx = self.slot(layer, j, c)
            dve.wait_ge(self.act_read, self.plan.read(it, (layer, j, c)))
            self.nc.vector.tensor_tensor(self.H[:, j, dst, c, LO], self.g[:, idx % self.NSLOT],
                                         self.H[:, j, dst, c, HI].bitcast(F32),
                                         ALU.subtract).then_inc(self.lo_ready, 1)

    def dve_add(self, dve, it, j, name, x):
        dve.wait_ge(self.filled, self.plan.filled(it, (name, j)))
        self.nc.vector.tensor_tensor(x, x, self.bank((name, j)), ALU.add).then_inc(self.dve_read, 1)

    def pe_outer_first(self, pe, it, j, parts):
        which = self.norms - 1
        self.pe_first(pe, it, which, j, ("a", "u"), (self.fw.w1, self.fw.w2), parts)

    def pe_outer_rest(self, pe, it, parts, following):
        w = self.fw
        pe.wait_ge(w.lo_done, 4)
        for j in range(2):
            self.pe_hidden(pe, it, j, "h1", "a", w.h1, 0, parts)
        pe.wait_ge(w.lo_done, 5)
        for j in range(2):
            self.pe_hidden(pe, it, j, "h2", "h1", w.h2, 1, parts)
        if following is not None:
            for j in range(2):
                self.pe_transpose_in(pe, following, 0, j)
        for j in range(2):
            self.pe_out(pe, it, j, "y", "h2", w.w3, 0, parts)
        for j in range(2):
            self.pe_transpose_out(pe, it, j, "yT", "y")

    def dve_outer_rest(self, dve, it, x, following, src, weight, subtract_mean, weights=[]):
        if following is not None:
            for j in range(2):
                self.dve_moments(dve, j, src[:, following * 2 + j])
        self.dve_hidden(dve, it, 0, "h1", 1)
        self.fw.dve_lo(dve, weights)
        if following is not None:
            dve.wait_ge(self.stats_ready, self.norm_count(following, 0, 1))
        self.dve_hidden(dve, it, 1, "h1", 1)
        if following is not None:
            for j in range(2):
                self.dve_aggregate(dve, j)
        self.dve_hidden(dve, it, 0, "h2", 0)
        if following is not None:
            for j in range(2):
                self.dve_normalise(dve, following, 0, j, src[:, following * 2 + j], subtract_mean)
        self.dve_hidden(dve, it, 1, "h2", 0)
        if following is not None:
            for j in range(2):
                self.dve_xT(dve, following, 0, j, weight)
        for j in range(2):
            self.dve_add(dve, it, j, "yT", x[:, it * 2 + j].rearrange("p i d -> p (i d)"))

    def act_outer(self, act, it, following, weight, weights=[]):
        w, last_norm = self.w, self.norms - 1
        self.act_first(act, it, 0, "a", w.scale[:, 0], 0)
        if last_norm:
            self.act_xT(act, it, last_norm, 1, None)
        self.fw.act_hi(act, weights[:1])
        self.act_first(act, it, 1, "a", w.scale[:, 0], 0)
        self.act_hidden(act, it, 0, "h1", w.scale[:, 2], 1)
        self.fw.act_hi(act, weights[1:])
        self.act_hidden(act, it, 1, "h1", w.scale[:, 2], 1)
        for j in range(2):
            self.act_hidden(act, it, j, "h2", w.scale[:, 3], 0)
        if following is not None:
            for j in range(2):
                self.act_xT(act, following, 0, j, weight)
        for j in range(2):
            self.act_out(act, it, j, "y", w.half_s3[:, 0:1])



def max_units(g):
    per_bank = {0: 4, 1: 2, 2: 1, 3: 1}
    return [(i, h, per_bank[i]) for i in range(NT) for h in range(0, HG, per_bank[i])]


CUTS = (1, 4, 2, 4)
TAIL = (1, 4, 1, 1, 2, 2)
BESIDE_0 = 2


def cut_units(g, cuts, lo, hi):
    return max_units(g)[sum(cuts[:lo]):sum(cuts[:hi])]


def prologue_uses():
    return ([(("hT",), "dve")] + [(("qkv", i), "dve") for i in range(NT)] + [(("qkT", n), "dve") for n in range(2)]
            + [(("max", 0, u), "dve") for u in max_units(0)] + [(("mT", 0), "act")]
            + [(("max", 1, u), "dve") for u in max_units(1)] + [(("mT", 1), "act")])


def maxima_uses(g, units):
    return [(("max", g, u), "dve") for u in units]


def attention_uses():
    uses = [(("hT",), "dve")] + [(("qkv", i), "dve") for i in range(NT)] + [(("qkT", n), "dve") for n in range(2)]
    uses += maxima_uses(2, max_units(2)) + maxima_uses(3, cut_units(3, CUTS, 0, 1)) + [(("mT", 2), "act")]
    uses += maxima_uses(3, cut_units(3, CUTS, 1, 3)) + [(("ctxT", 0), "dve")]
    uses += maxima_uses(3, cut_units(3, CUTS, 3, 4))
    uses += maxima_uses(0, cut_units(0, CUTS, 0, 1)) + [(("mT", 3), "act")]
    uses += maxima_uses(0, cut_units(0, CUTS, 1, 3)) + [(("ctxT", 1), "dve")]
    uses += maxima_uses(0, cut_units(0, CUTS, 3, 4))
    uses += maxima_uses(1, cut_units(1, TAIL, 0, 1)) + [(("mT", 0), "act")]
    uses += maxima_uses(1, cut_units(1, TAIL, 1, 3)) + [(("ctxT", 2), "dve")]
    uses += maxima_uses(1, cut_units(1, TAIL, 3, 4)) + [(("ctxT", 3), "dve")]
    uses += maxima_uses(1, cut_units(1, TAIL, 4, 5)) + [(("cT",), "dve")]
    uses += maxima_uses(1, cut_units(1, TAIL, 5, 6))
    return uses + [(("wo",), "act"), (("mT", 1), "act"), (("attn",), "dve")]


def last_uses():
    uses = maxima_uses(2, max_units(2)) + maxima_uses(3, max_units(3)[:4]) + [(("mT", 2), "act")]
    uses += maxima_uses(3, max_units(3)[4:]) + [(("mT", 3), "act")] + [(("ctxT", g), "dve") for g in range(NG)]
    return uses + [(("cT",), "dve"), (("wo",), "act"), (("attn",), "dve")]


RING = [4, 5, 6]
CTX_BANK = 7
MASK_STEPS = 8
UNITS = 5
NV = 16
EXT_DMAS = 2 * NPART * NPART + 1


class AttentionBuffers:
    def __init__(self, sb):
        self.wa = sb("wa", [P, 2, 4 * D], F32R)
        self.hn = sb("hn", [P, NT, D], F32)
        self.hT = sb("hT", [P, 2, S], F32R)
        self.stats = sb("stats", [P, NT, 6], F32)
        self.mv = sb("mv", [P, NT, 2], F32)
        self.small = sb("small", [P, 4, NT], F32)
        self.rstd = sb("rstd", [P, NT], F32)
        self.both = sb("both", [P, NT], F32)
        self.cos_part = sb("cos_part", [P, 2, 2 * D], F32)
        self.sin_part = sb("sin_part", [P, 2, 2 * D], F32)
        self.qk = sb("qk", [P, NT, 2, DK, NH], F32)
        self.part = sb("part", [P, 2, NPART, S], BF16)
        self.rest = sb("rest", [P, 2, S], F32)
        self.ext = [[sb(f"{n}_ext{p}", [NE, NH, S], BF16) for n in ("q", "k")] for p in range(2)]
        self.V = [sb(f"V{p}", [P, NT, NH, NV], F32) for p in range(2)]
        self.zero = sb("zero", [P, 1], F32)
        self.spare = sb("spare", [P, 1], F32)
        self.neg_max = sb("neg_max", [P, 2, NT, HG], F32)
        self.neg_max2 = sb("neg_max2", [P, NT, 2, HG], BF16)
        self.max_rows = sb("max_rows", [2 * HG, S], BF16)
        self.PT = sb("PT", [P, 2, UNITS, 2 * S], F32)
        self.ctxs = sb("ctxs", [P, 2, S], F32)
        self.recip = sb("recip", [P, 2, NT, HG], F32)
        self.ctxn = sb("ctxn", [P, NT, NH, DK], F32)
        self.cT = sb("cT", [P, 2, S], F32R)
        self.aT = sb("aT", [P, S], F32)
        self.ident16 = sb("ident16", [P, P], BF16)
        self.mask16 = sb("mask16", [P, P], BF16)
        self.fill16 = sb("fill16", [P, 2, P], BF16)
        self.tab = sb("tab", [P, 2, NT, DK], F32)


class Attention:

    def __init__(self, nc, bufs, psum, w, x, y2, plan, sem, shared, first):
        self.nc, self.t, self.psum, self.w, self.x, self.y2, self.plan = nc, bufs, psum, w, x, y2, plan
        self.first = first
        self.ext_loaded, self.m_loaded = shared
        self.s_filled = sem("filled")
        self.s_act_read = sem("act_read")
        self.s_dve_read = sem("dve_read")
        self.s_stats_ready = sem("stats_ready")
        self.s_moments = sem("moments")
        self.s_pool_step = sem("pool_step")
        self.s_factors = sem("factors")
        self.s_hn_ready = sem("hn_ready")
        self.s_hT_hi = sem("hT_hi")
        self.s_rope_step = sem("rope_step")
        self.s_qk_hi = sem("qk_hi")
        self.s_mid_ready = sem("mid_ready")
        self.s_parts_ready = sem("parts_ready")
        self.s_max_hi = sem("max_hi")
        self.s_max_ready = sem("max_ready")
        self.s_scores = sem("scores")
        self.s_exps = sem("exps")
        self.s_masks = sem("masks")
        self.s_ctx = sem("ctx")
        self.s_ctx_read = sem("ctx_read")
        self.s_recips = sem("recips")
        self.s_cT_hi = sem("cT_hi")
        self.s_x_done = sem("x_done")

    def bank(self, name):
        return self.psum[:, self.plan.bank(name), :]

    def pe_bank(self, pe, b, name):
        who, value = self.plan.last_user(b, name)
        pe.wait_ge(self.s_act_read if who == "act" else self.s_dve_read, value)
        return self.bank(name)

    def dve_moments(self, dve, b, s):
        for i in range(NT):
            last = self.nc.vector.bn_stats(self.t.stats[:, i], self.x[:, s, i, :])
        last.then_inc(self.s_stats_ready, 1)

    def dve_aggregate(self, dve, b):
        for i in range(NT):
            last = self.nc.vector.bn_aggr(self.t.mv[:, i], self.t.stats[:, i])
        last.then_inc(self.s_moments, 1)

    def pool_factors(self, pool, b):
        t, g, n = self.t, self.nc.gpsimd, 6
        pool.wait_ge(self.s_moments, b + 1)
        var = t.mv[:, :, 1]
        g.tensor_tensor(t.small[:, 0], var, self.w.eps[:, :], ALU.add).then_inc(self.s_pool_step, 1)
        pool.wait_ge(self.s_pool_step, b * n + 1)
        g.tensor_tensor(t.rstd[:, :], t.small[:, 0], self.w.minus_half[:, :], ALU.pow).then_inc(self.s_pool_step, 1)
        pool.wait_ge(self.s_pool_step, b * n + 2)
        g.tensor_tensor(t.small[:, 1], var, t.rstd[:, :], ALU.mult).then_inc(self.s_pool_step, 1)
        pool.wait_ge(self.s_pool_step, b * n + 3)
        g.tensor_tensor(t.small[:, 2], t.small[:, 1], t.rstd[:, :], ALU.mult).then_inc(self.s_pool_step, 1)
        pool.wait_ge(self.s_pool_step, b * n + 4)
        g.tensor_tensor(t.small[:, 1], t.small[:, 2], self.w.eps[:, :], ALU.add).then_inc(self.s_pool_step, 1)
        pool.wait_ge(self.s_pool_step, b * n + 5)
        g.tensor_tensor(t.small[:, 3], t.small[:, 1], self.w.minus_half[:, :], ALU.pow).then_inc(self.s_pool_step, 1)
        pool.wait_ge(self.s_pool_step, b * n + 6)
        g.tensor_tensor(t.both[:, :], t.small[:, 3], t.rstd[:, :], ALU.mult).then_inc(self.s_factors, 1)

    def dve_normalise(self, dve, b, s):
        t = self.t
        dve.wait_ge(self.s_factors, b + 1)
        for i in range(NT):
            last = self.nc.vector.tensor_scalar(t.hn[:, i], self.x[:, s, i, :], t.mv[:, i, 0:1], t.both[:, i:i + 1],
                                                ALU.subtract, ALU.mult)
        last.then_inc(self.s_hn_ready, 1)

    def dve_layernorm(self, dve, b, s):
        t = self.t
        for i in range(NT):
            self.nc.vector.tensor_scalar(self.y2[:, s, i, :], self.x[:, s, i, :], t.mv[:, i, 0:1],
                                         t.rstd[:, i:i + 1], ALU.subtract, ALU.mult)

    def pe_hT(self, pe, b):
        bank = self.pe_bank(pe, b, ("hT",))
        pe.wait_ge(self.s_hn_ready, b + 1)
        for i in range(NT):
            last = pe.transpose(bank[:, i * P:(i + 1) * P], self.t.hn[:, i, :], self.w.ident[:, :])
        last.then_inc(self.s_filled, 1)

    def act_hT(self, act, b):
        act.wait_ge(self.s_filled, self.plan.filled(b, ("hT",)))
        act.activation(self.t.hT[:, HI], self.bank(("hT",)), ACT.Copy,
                       scale=self.w.norms[:, 0:1]).then_inc(self.s_hT_hi, 1)

    def dve_hT(self, dve, b):
        t, bank, weight = self.t, self.bank(("hT",)), self.w.norms[:, 0:1]
        dve.wait_ge(self.s_hT_hi, b + 1)
        self.nc.vector.scalar_tensor_tensor(t.hT[:, LO], bank, weight, t.hT[:, HI].bitcast(F32), ALU.mult,
                                            ALU.subtract).then_inc(self.s_dve_read, 1)

    def pe_qkv(self, pe, b, i):
        t = self.t
        if i == 0:
            pe.wait_ge(self.s_dve_read, self.plan.read(b, ("hT",)))
        bank = self.pe_bank(pe, b, ("qkv", i))
        for n, (wp, dp) in enumerate(SPLIT3):
            last = pe.matmul(bank[:, 0:3 * D], t.hT[:, dp, i * P:(i + 1) * P], t.wa[:, wp, 0:3 * D],
                             start=(n == 0), stop=(n == len(SPLIT3) - 1))
        last.then_inc(self.s_filled, 1)

    def dve_rope(self, dve, b, par):
        t, v = self.t, self.nc.vector
        for i in range(NT):
            bank, slot = self.bank(("qkv", i)), i % 2
            qk = bank[:, 0:2 * D].rearrange("p (n d) -> p n d", d=DK)
            dve.wait_ge(self.s_filled, self.plan.filled(b, ("qkv", i)))
            if i >= 2:
                dve.wait_ge(self.s_dve_read, self.plan.read(b, ("qkv", i - 2)))
            cos = t.tab[:, 0, i:i + 1, :].to_broadcast([P, 2 * NH, DK])
            v.tensor_tensor(t.cos_part[:, slot].rearrange("p (n d) -> p n d", d=DK), qk, cos, ALU.mult)
            sin = t.tab[:, 1, i:i + 1, :].to_broadcast([P, 2 * NH, DK]).rearrange("p n (d e) -> p n d e", e=2)
            swapped = t.sin_part[:, slot].rearrange("p (n d e) -> p n d e", d=DK // 2, e=2)
            v.tensor_tensor(swapped[:, :, :, ::-1],
                            bank[:, 0:2 * D].rearrange("p (n d e) -> p n d e", d=DK // 2, e=2), sin,
                            ALU.mult).then_inc(self.s_rope_step, 1)
            dve.wait_ge(self.s_rope_step, b * NT + (i + 1))
            v.tensor_tensor(t.qk[:, i].rearrange("p q d h -> p q h d"),
                            t.cos_part[:, slot].rearrange("p (q h d) -> p q h d", q=2, d=DK),
                            t.sin_part[:, slot].rearrange("p (q h d) -> p q h d", q=2, d=DK), ALU.add)
            v.tensor_copy(t.V[par][:, i, :, 0:DK],
                          bank[:, 2 * D:3 * D].rearrange("p (h d) -> p h d", d=DK)).then_inc(self.s_dve_read, 1)

    def pe_qkT(self, pe, b):
        for n in range(2):
            bank = self.pe_bank(pe, b, ("qkT", n))
            pe.wait_ge(self.s_dve_read, self.plan.read(b, ("qkv", NT - 1)))
            for i in range(NT):
                last = pe.transpose(bank[:, i * P:(i + 1) * P],
                                    self.t.qk[:, i, n].rearrange("p d h -> p (d h)"), self.w.ident[:, :])
            last.then_inc(self.s_filled, 1)

    def act_qkT(self, act, b, loads_before):
        for n in range(2):
            act.wait_ge(self.s_filled, self.plan.filled(b, ("qkT", n)))
            if loads_before is not None:
                act.wait_ge(self.ext_loaded, loads_before)
            act.activation(self.t.part[:, n, 0], self.bank(("qkT", n)), ACT.Copy).then_inc(self.s_qk_hi, 1)

    def dve_rest(self, dve, b):
        for n in range(2):
            dve.wait_ge(self.s_qk_hi, b * 2 + (n + 1))
            self.nc.vector.tensor_tensor(self.t.rest[:, n], self.bank(("qkT", n)), self.t.part[:, n, 0],
                                         ALU.subtract).then_inc(self.s_dve_read, 1)

    def act_parts(self, act, b, n):
        act.wait_ge(self.s_dve_read, self.plan.read(b, ("qkT", n)))
        act.activation(self.t.part[:, n, 1], self.t.rest[:, n], ACT.Copy).then_inc(self.s_mid_ready, 1)

    def pool_parts(self, pool, b):
        t = self.t
        for n in range(2):
            pool.wait_ge(self.s_mid_ready, b * 2 + (n + 1))
            self.nc.gpsimd.tensor_tensor(t.part[:, n, 2], t.rest[:, n], t.part[:, n, 1],
                                         ALU.subtract).then_inc(self.s_parts_ready, 1)

    def load_ext(self, queue, b, par, which):
        t = self.t
        for m, ready in enumerate((self.s_qk_hi, self.s_mid_ready, self.s_parts_ready)):
            for n in which:
                queue.wait_ge(ready, b * 2 + (n + 1))
                for other in range(NPART):
                    row = DK * (NPART * other + m if n == 0 else NPART * m + other)
                    queue.dma_start(t.ext[par][n][row:row + DK, :, :], t.part[:, n, m, :]).then_inc(self.ext_loaded, 16)
                if (m, n) == (0, 0):
                    queue.dma_start(t.ext[par][0][M_ROW:M_ROW + 2, :, :],
                                    t.fill16[:, 0, :]).then_inc(self.ext_loaded, 16)

    def pe_max(self, pe, b, g, par, loads, units=None):
        t = self.t
        q_ext, k_ext = t.ext[par]
        if loads is not None:
            pe.wait_ge(self.ext_loaded, loads)
        for unit in max_units(g) if units is None else units:
            i, h0, nh = unit
            bank, width = self.pe_bank(pe, b, ("max", g, unit)), (i + 1) * P
            for k in range(nh):
                h = HG * g + h0 + k
                pe.matmul(bank[:, k * width:(k + 1) * width], q_ext[:, h, i * P:(i + 1) * P], k_ext[:, h, 0:width],
                          start=True, stop=False)
                last = pe.matmul(bank[:, k * width + i * P:(k + 1) * width], t.ident16[:, :], t.mask16[:, :],
                                 start=False, stop=True)
            last.then_inc(self.s_filled, 1)

    def dve_max(self, dve, b, g, units=None):
        t = self.t
        for unit in max_units(g) if units is None else units:
            i, h0, nh = unit
            dve.wait_ge(self.s_filled, self.plan.filled(b, ("max", g, unit)))
            scores = self.bank(("max", g, unit))[:, 0:nh * (i + 1) * P].rearrange("p (h k) -> p h k", h=nh)
            self.nc.vector.tensor_reduce(t.neg_max[:, g % 2, i, h0:h0 + nh], scores, AX_X, ALU.max,
                                         negate=True).then_inc(self.s_dve_read, 1)

    def dve_max_parts(self, dve, b, g, slot):
        t, v = self.t, self.nc.vector
        n = b * NG + slot
        dve.wait_ge(self.s_dve_read, self.plan.read(b, ("max", g, max_units(g)[-1])))
        v.tensor_copy(t.neg_max2[:, :, 0], t.neg_max[:, g % 2]).then_inc(self.s_max_hi, 1)
        dve.wait_ge(self.s_max_hi, n + 1)
        v.tensor_tensor(t.neg_max2[:, :, 1], t.neg_max[:, g % 2], t.neg_max2[:, :, 0],
                        ALU.subtract).then_inc(self.s_max_ready, 1)

    def pe_mT(self, pe, b, g, slot):
        bank = self.pe_bank(pe, b, ("mT", g)).bitcast(BF16)
        pe.wait_ge(self.s_max_ready, b * NG + (slot + 1))
        for i in range(NT):
            last = pe.transpose(bank[0:2 * HG, i * P:(i + 1) * P],
                                self.t.neg_max2[:, i].rearrange("p n h -> p (n h)"), self.t.ident16[:, :])
        last.then_inc(self.s_filled, 1)

    def act_mT(self, act, b, g, loaded_before, par):
        act.wait_ge(self.s_filled, self.plan.filled(b, ("mT", g)))
        if loaded_before is not None:
            act.wait_ge(self.m_loaded, loaded_before)
        act.activation(self.t.max_rows[:, :], self.bank(("mT", g)).bitcast(BF16)[0:2 * HG, 0:S],
                       ACT.Copy).then_inc(self.s_act_read, 1)
        act.wait_ge(self.s_act_read, self.plan.read(b, ("mT", g)))
        act.dma_start(self.t.ext[par][0][M_ROW:M_ROW + 2, HG * g:HG * (g + 1), :],
                      self.t.max_rows[:, :]).then_inc(self.m_loaded, 16)

    def pieces(self, u):
        if u < HG:
            return [(u, 0, 0), (u, 1, S), (u, 3, S + 3 * P)]
        return [(h, 2, h * 2 * P) for h in range(HG)]

    def pe_scores(self, pe, b, g, par, units=range(UNITS)):
        q_ext, k_ext = self.t.ext[par]
        pe.wait_ge(self.m_loaded, (b + self.first) * (NG * 16) + (g + 1) * 16)
        for u in units:
            n = UNITS * g + u
            pe.wait_ge(self.s_exps, b * (NG * UNITS) + (n + 1))
            both = self.psum[:, 2 * (n % 2):2 * (n % 2) + 2, :].rearrange("p n s -> p (n s)")
            for h, j, col in self.pieces(u):
                width = S - j * P
                last = pe.matmul(both[:, col:col + width], k_ext[:, HG * g + h, j * P:(j + 1) * P],
                                 q_ext[:, HG * g + h, j * P:S], start=True, stop=True)
            last.then_inc(self.s_scores, 1)

    def act_exp(self, act, b, g, units=range(UNITS)):
        t = self.t
        for u in units:
            n = UNITS * g + u
            if u == 0:
                act.wait_ge(self.s_ctx, b * NG + (g + 3))
            act.wait_ge(self.s_scores, b * (NG * UNITS) + (n + 1))
            act.activation(t.PT[:, g % 2, u], self.psum[:, 2 * (n % 2):2 * (n % 2) + 2, :].rearrange("p n s -> p (n s)"),
                           ACT.Exp, scale=SCALE).then_inc(self.s_exps, 1)

    def pool_mask(self, pool, b, g):
        t = self.t
        heads = t.PT[:, g % 2, 0:HG, :].rearrange("p h (n q) -> p h n q", q=P)
        third = t.PT[:, g % 2, HG, :].rearrange("p (h q) -> p h q", h=HG)[:, :, 0:P]
        stages = [(2, [heads[:, 0:2, 0:2 * NT:NT, :], heads[:, 0:2, 2 * NT - 1, :]]),
                  (4, [heads[:, 2:4, 0:2 * NT:NT, :], heads[:, 2:4, 2 * NT - 1, :]]), (5, [third])]
        n = b * (NG * MASK_STEPS) + MASK_STEPS * g + 1
        for units, views in stages:
            pool.wait_ge(self.s_exps, b * (NG * UNITS) + (UNITS * g + units + 2))
            pool.wait_ge(self.s_masks, n)
            self.nc.gpsimd.tensor_tensor(t.spare[:, :], t.zero[:, :], t.zero[:, :],
                                         ALU.add).then_inc(self.s_masks, 1)
            for v in views:
                repeated = [[0, k] for k in v.shape[1:-1]]
                self.nc.gpsimd.affine_select(out=v, in_=v, compare_op=ALU.is_ge, fill=0.0, base=0,
                                             pattern=repeated + [[1, P]], channel_multiplier=-1).then_inc(self.s_masks, 1)
            n = n + (1 + len(views))

    def pe_context(self, pe, b, g, par, j):
        t = self.t
        if j == 0:
            pe.wait_ge(self.s_masks, b * (NG * MASK_STEPS) + (MASK_STEPS * (g + 1) + 1))
            pe.wait_ge(self.s_ctx_read, b * NG + (g + 1))
        for h in range(HG):
            unit, col = {0: (h, 0), 1: (h, S), 3: (h, S + 3 * P), 2: (HG, h * 2 * P)}[j]
            last = pe.matmul(self.psum[32 * h:32 * h + NV, CTX_BANK, j * P:S], t.V[par][:, j, HG * g + h, :],
                             t.PT[:, g % 2, unit, col:col + S - j * P], start=(j == 0), stop=(j == NT - 1))
        if j == NT - 1:
            last.then_inc(self.s_ctx, 1)

    def act_context(self, act, b, g):
        act.wait_ge(self.s_ctx, b * NG + (g + 5))
        act.activation(self.t.ctxs[:, g % 2], self.psum[:, CTX_BANK, :], ACT.Copy).then_inc(self.s_ctx_read, 1)

    def pe_ctxT(self, pe, b, g):
        bank = self.pe_bank(pe, b, ("ctxT", g))
        pe.wait_ge(self.s_ctx_read, b * NG + (g + 2))
        for i in range(NT):
            last = pe.transpose(bank[:, i * P:(i + 1) * P], self.t.ctxs[:, g % 2, i * P:(i + 1) * P], self.w.ident[:, :])
        last.then_inc(self.s_filled, 1)

    def dve_ctxT(self, dve, b, g):
        t, v = self.t, self.nc.vector
        ctx = self.bank(("ctxT", g)).rearrange("p (i h c) -> p i h c", i=NT, h=HG)
        dve.wait_ge(self.s_filled, self.plan.filled(b, ("ctxT", g)))
        v.reciprocal(t.recip[:, g % 2], ctx[:, :, :, DK]).then_inc(self.s_recips, 1)
        dve.wait_ge(self.s_recips, b * NG + (g + 1))
        v.tensor_tensor(t.ctxn[:, :, HG * g:HG * (g + 1), :], ctx[:, :, :, 0:DK],
                        t.recip[:, g % 2].unsqueeze(3).to_broadcast([P, NT, HG, DK]),
                        ALU.mult).then_inc(self.s_dve_read, 1)

    def pe_cT(self, pe, b):
        bank = self.pe_bank(pe, b, ("cT",))
        pe.wait_ge(self.s_dve_read, self.plan.read(b, ("ctxT", NG - 1)))
        for i in range(NT):
            last = pe.transpose(bank[:, i * P:(i + 1) * P], self.t.ctxn[:, i].rearrange("p h d -> p (h d)"),
                                self.w.ident[:, :])
        last.then_inc(self.s_filled, 1)

    def act_cT(self, act, b):
        act.wait_ge(self.s_filled, self.plan.filled(b, ("cT",)))
        act.activation(self.t.cT[:, HI], self.bank(("cT",)), ACT.Copy).then_inc(self.s_cT_hi, 1)

    def dve_cT(self, dve, b):
        t, bank = self.t, self.bank(("cT",))
        dve.wait_ge(self.s_cT_hi, b + 1)
        self.nc.vector.tensor_tensor(t.cT[:, LO], bank, t.cT[:, HI].bitcast(F32), ALU.subtract)\
            .then_inc(self.s_dve_read, 1)

    def pe_wo(self, pe, b):
        t = self.t
        bank = self.pe_bank(pe, b, ("wo",))
        pe.wait_ge(self.s_dve_read, self.plan.read(b, ("cT",)))
        product(pe, bank, lambda k, p: t.wa[:, p, 3 * D:4 * D], lambda k, p: t.cT[:, p], 1,
                SPLIT3).then_inc(self.s_filled, 1)

    def act_wo(self, act, b):
        act.wait_ge(self.s_filled, self.plan.filled(b, ("wo",)))
        act.activation(self.t.aT[:, :], self.bank(("wo",)), ACT.Copy).then_inc(self.s_act_read, 1)

    def pe_attn(self, pe, b):
        bank = self.pe_bank(pe, b, ("attn",))
        pe.wait_ge(self.s_act_read, self.plan.read(b, ("wo",)))
        for i in range(NT):
            last = pe.transpose(bank[:, i * P:(i + 1) * P], self.t.aT[:, i * P:(i + 1) * P], self.w.ident[:, :])
        last.then_inc(self.s_filled, 1)

    def dve_attn(self, dve, b, s):
        dve.wait_ge(self.s_filled, self.plan.filled(b, ("attn",)))
        y2, xs = (v[:, s].rearrange("p i d -> p (i d)") for v in (self.y2, self.x))
        self.nc.vector.tensor_tensor(y2, y2, self.bank(("attn",)), ALU.add).then_inc(self.s_dve_read, 1)
        dve.wait_ge(self.s_dve_read, self.plan.read(b, ("attn",)))
        self.nc.vector.tensor_tensor(xs, xs, y2, ALU.add).then_inc(self.s_x_done, 1)


class FfnWeights:

    def __init__(self, nc, sb, sem, drams):
        self.nc = nc
        self.w1, self.w2 = sb("w1", [P, 2, HID], F32R), sb("w2", [P, 2, HID], F32R)
        self.h1, self.h2 = sb("h1", [P, 2, KC, HID], F32R), sb("h2", [P, 2, KC, HID], F32R)
        self.w3 = sb("w3", [P, 2, KC, D], F32R)
        raw12 = sb("raw12", [P, 2, HID], F32)
        rawh = [sb(f"rawh{n}", [P, KC, HID], F32) for n in range(2)]
        raw3 = sb("raw3", [P, KC, D], F32)
        w12, h, w3 = drams
        self.pieces = [(w12[0], raw12[:, 0], self.w1), (w12[1], raw12[:, 1], self.w2),
                       (w3.rearrange("(k p) o -> p k o", p=P), raw3[:, :, :], self.w3),
                       (h[0].rearrange("(k p) o -> p k o", p=P), rawh[0][:, :, :], self.h1),
                       (h[1].rearrange("(k p) o -> p k o", p=P), rawh[1][:, :, :], self.h2)]
        self.loaded = [sem(f"w_loaded{n}") for n in range(len(self.pieces))]
        self.hi_done, self.lo_done = sem("w_hi_done"), sem("w_lo_done")

    def sp_load(self, sp, which):
        for n in which:
            src, raw, _ = self.pieces[n]
            sp.dma_start(raw, src).then_inc(self.loaded[n], 16)

    def act_hi(self, act, which):
        for n in which:
            _, raw, split = self.pieces[n]
            act.wait_ge(self.loaded[n], 16)
            act.activation(split[:, HI], raw, ACT.Copy).then_inc(self.hi_done, 1)

    def dve_lo(self, dve, which):
        for n in which:
            _, raw, split = self.pieces[n]
            dve.wait_ge(self.hi_done, n + 1)
            self.nc.vector.tensor_tensor(split[:, LO], raw, split[:, HI].bitcast(F32),
                                         ALU.subtract).then_inc(self.lo_done, 1)


def bass_macaron(nc, x_in, ffn_w12, ffn_h, ffn_w3, ffn_scales, ffn_s3, attn_qkvo, attn_w13, attn_w2,
                 attn_norms, tables, out):
    half = B // 2
    with ExitStack() as ctx:
        def sem(name):
            return ctx.enter_context(nc.semaphore(name))

        def keep(name, shape, dt):
            return ctx.enter_context(nc.sbuf_tensor(name, shape, dt))

        class Constants:
            scale = keep("scale", [P, 4, KC], F32)
            half_s3 = keep("half_s3", [P, 1], F32)
            norms = keep("norms", [P, 2], F32)
            ident = keep("ident", [P, P], F32)
            minus_half = keep("minus_half", [P, NT], F32)
            eps = keep("eps", [P, NT], F32)

        w = Constants()
        ones = keep("ones", [P, 1], F32)
        lo_sums = keep("lo_sums", [P, 8], F32)
        flag = keep("flag", [1, 1], I32)
        x = keep("x", [P, B, NT, D], F32)
        y2 = keep("y2", [P, B, NT, D], F32)
        iw = [keep(f"iw{n}", [P, 2, HID], F32R) for n in range(3)]
        psum = ctx.enter_context(nc.psum_tensor("psum", [P, 8, S], F32))
        drams = (ffn_w12, ffn_h, ffn_w3)

        with ExitStack() as scope:
            def sb(name, shape, dt):
                return scope.enter_context(nc.sbuf_tensor("b1_" + name, shape, dt))

            def sem1(name):
                return sem("b1_" + name)

            plan = BankPlan(ffn_uses(), FFN_RING)
            fw = FfnWeights(nc, sb, sem1, drams)
            f = Ffn(nc, sb, sem1, psum, w, fw, plan, inner=False)
            x_loaded = [sem(f"x_loaded{n}") for n in range(2)]
            const_loaded, const_set, w_sum = sem("const_loaded"), sem("const_set"), sem("w_sum")
            sums_added, flag_sum, flag_ready = sem("sums_added"), sem("flag_sum"), sem("flag_ready")
            pieces = list(range(5))

            def x_view(lo, hi):
                return x_in[lo:hi].rearrange("b (i p) d -> p b i d", p=P)

            with nc.Block() as block:
                @block.sync
                def _(sp):
                    fw.sp_load(sp, [0])
                    sp.dma_start(x[:, 0:2], x_view(0, 2)).then_inc(x_loaded[0], 16)
                    fw.sp_load(sp, pieces[1:])
                    sp.dma_start(w.ident[:, :], tables[:, 0:P]).then_inc(const_loaded, 16)
                    sp.dma_start(w.scale[:, :, :], ffn_scales).then_inc(const_loaded, 16)
                    sp.dma_start(w.half_s3[:, :], ffn_s3).then_inc(const_loaded, 16)
                    sp.dma_start(w.norms[:, :], attn_norms).then_inc(const_loaded, 16)
                    sp.dma_start(x[:, 2:B], x_view(2, B)).then_inc(x_loaded[1], 16)

                @block.gpsimd
                def _(pool):
                    pool.wait_ge(const_set, 1)
                    with pool.Fori(0, half) as it:
                        for j in range(2):
                            f.pool_rstd(pool, it, 0, j, mean_square=False)

                @block.scalar
                def _(act):
                    act.sem_inc(f.act_read, plan.per["act"])
                    act.wait_ge(const_set, 1)
                    fw.act_hi(act, [0])
                    for n, (_, raw, split) in enumerate(fw.pieces):
                        fw.act_hi(act, pieces[n + 1:n + 2])
                        if n == len(fw.pieces) - 2:
                            for j in range(2):
                                f.act_xT(act, 0, 0, j, None)
                        act.wait_ge(fw.lo_done, n + 1)
                        act.activation(raw, split[:, LO].bitcast(F32), ACT.Abs,
                                       accum_out=lo_sums[:, n:n + 1]).then_inc(w_sum, 1)
                    act.wait_ge(const_set, 2)
                    with act.Fori(0, half - 1) as it:
                        f.act_outer(act, it, it + 1, None)
                    f.act_outer(act, half - 1, None, None)

                @block.vector
                def _(dve):
                    dve.sem_inc(f.dve_read, plan.per["dve"])
                    dve.sem_inc(f.xT_read, 2)
                    nc.vector.memset(w.minus_half[:, :], -0.5)
                    nc.vector.memset(w.eps[:, :], EPS)
                    nc.vector.memset(lo_sums[:, :], 0.0)
                    nc.vector.memset(ones[:, :], 1.0).then_inc(const_set, 1)
                    fw.dve_lo(dve, [0])
                    dve.wait_ge(x_loaded[0], 16)
                    for j in range(2):
                        f.dve_moments(dve, j, x[:, j])
                    fw.dve_lo(dve, [1])
                    for j in range(2):
                        dve.wait_ge(f.stats_ready, j + 1)
                        f.dve_aggregate(dve, j)
                    fw.dve_lo(dve, [2])
                    for j in range(2):
                        f.dve_normalise(dve, 0, 0, j, x[:, j], True)
                    fw.dve_lo(dve, [3])
                    for j in range(2):
                        f.dve_xT(dve, 0, 0, j, None)
                    fw.dve_lo(dve, [4])
                    dve.wait_ge(const_loaded, 64)
                    nc.vector.tensor_scalar(w.half_s3[:, :], w.half_s3[:, :], 0.5, None,
                                            ALU.mult).then_inc(const_set, 1)
                    dve.wait_ge(w_sum, len(pieces))
                    nc.vector.tensor_reduce(lo_sums[:, 7:8], lo_sums[:, 0:5], AX_X,
                                            ALU.add).then_inc(sums_added, 1)
                    dve.wait_ge(flag_sum, 1)
                    nc.vector.tensor_scalar(flag[:, :], psum[0:1, 0, 0:1], 0.0, None,
                                            ALU.not_equal).then_inc(flag_ready, 1)


                    def pair(it, following):
                        for j in range(2):
                            f.dve_first(dve, it, j, "a", "u", w.scale[:, 1], 0)
                        f.dve_outer_rest(dve, it, x, following, x, None, True)

                    dve.wait_ge(x_loaded[1], 16)
                    with dve.Fori(0, half - 1) as it:
                        pair(it, it + 1)
                    pair(half - 1, None)

                @block.tensor
                def _(pe):
                    pe.wait_ge(const_loaded, 64)
                    for j in range(2):
                        f.pe_transpose_in(pe, 0, 0, j)
                    pe.wait_ge(sums_added, 1)
                    pe.matmul(psum[0:1, 0, 0:1], lo_sums[:, 7:8], ones[:, :], start=True,
                              stop=True).then_inc(flag_sum, 1)
                    pe.wait_ge(flag_ready, 1)
                    has_lo = pe.value_load(flag[0:1, 0:1])

                    def pair(it, following, parts):
                        for j in range(2):
                            f.pe_outer_first(pe, it, j, parts)
                        f.pe_outer_rest(pe, it, parts, following)

                    def loop(parts):
                        with pe.Fori(0, half - 1) as it:
                            pair(it, it + 1, parts)
                        pair(half - 1, None, parts)

                    with pe.If(has_lo != 0):
                        loop(ALL4)
                    with pe.Else():
                        loop(EXACT_W)

        with ExitStack() as scope:
            def sb(name, shape, dt):
                return scope.enter_context(nc.sbuf_tensor("b2_" + name, shape, dt))

            bufs = AttentionBuffers(sb)
            raw = sb("raw", [P, 4 * D], F32)
            raw_mask = sb("raw_mask", [P, P], F32)
            raw_i = [sb(f"raw_i{n}", [P, HID], F32) for n in range(2)] + [bufs.aT]
            i_loaded, i_hi = sem("i_loaded"), sem("i_hi")
            shared = sem("ext_loaded"), sem("m_loaded")
            loads = EXT_DMAS * 16

            def attention(prefix, uses, first):
                return Attention(nc, bufs, psum, w, x, y2, BankPlan(uses, RING),
                                 lambda n: sem(prefix + n), shared, first)

            a = attention("b2a_", prologue_uses(), 0)
            wa_loaded, tab_loaded, wa_hi, wa_lo, set16 = (sem("wa_loaded"), sem("tab_loaded"), sem("wa_hi"),
                                                          sem("wa_lo"), sem("set16"))
            ones_loaded, zeros_set, zeros_loaded = sem("ones_loaded"), sem("zeros_set"), sem("zeros_loaded")
            zeros = bufs.ctxs[0:(NE - M_ROW - 2) * NH * S // (4 * S), :, :].rearrange("p n s -> p (n s)").bitcast(BF16)
            with nc.Block() as block:
                @block.sync
                def _(sp):
                    sp.dma_start(raw[:, :], attn_qkvo).then_inc(wa_loaded, 16)
                    sp.dma_start(raw_mask[:, :], tables[:, P:2 * P]).then_inc(tab_loaded, 16)
                    sp.dma_start(bufs.tab[:, :, :, :].rearrange("p n i d -> p (n i d)"),
                                 tables[:, 2 * P:]).then_inc(tab_loaded, 16)
                    for n in range(2):
                        sp.dma_start(raw_i[n][:, :], attn_w13[n]).then_inc(i_loaded, 16)
                    sp.dma_start(raw_i[2].rearrange("p (k o) -> p k o", k=KC),
                                 attn_w2.rearrange("(k p) o -> p k o", p=P)).then_inc(i_loaded, 16)
                    sp.wait_ge(zeros_set, 1)
                    for par in range(2):
                        for n in range(2):
                            sp.dma_start(bufs.ext[par][n][M_ROW + 2:NE, :, :], zeros).then_inc(zeros_loaded, 16)
                    sp.wait_ge(set16, 2)
                    for par in range(2):
                        sp.dma_start(bufs.ext[par][1][M_ROW:M_ROW + 2, :, :],
                                     bufs.fill16[:, 1, :]).then_inc(ones_loaded, 16)
                    a.load_ext(sp, 0, 0, [0])
                    sp.wait_ge(shared[1], 32)
                    sp.wait_ge(zeros_loaded, 64)

                @block.gpsimd
                def _(pool):
                    a.pool_factors(pool, 0)
                    a.pool_parts(pool, 0)
                    a.pool_factors(pool, 1)

                @block.scalar
                def _(act):
                    act.sem_inc(a.s_act_read, a.plan.per["act"])
                    act.wait_ge(wa_loaded, 16)
                    act.activation(bufs.wa[:, HI], raw[:, :], ACT.Copy).then_inc(wa_hi, 1)
                    a.act_hT(act, 0)
                    a.act_qkT(act, 0, None)
                    for n in range(2):
                        a.act_parts(act, 0, n)
                    a.load_ext(act, 0, 0, [1])
                    act.wait_ge(i_loaded, 48)
                    for n in range(3):
                        act.activation(iw[n][:, HI], raw_i[n][:, :], ACT.Copy).then_inc(i_hi, 1)
                    a.act_mT(act, 0, 0, None, 0)
                    a.act_mT(act, 0, 1, 16, 0)

                @block.vector
                def _(dve):
                    v = nc.vector
                    dve.sem_inc(a.s_dve_read, a.plan.per["dve"])
                    a.dve_moments(dve, 0, 0)
                    dve.wait_ge(a.s_stats_ready, 1)
                    a.dve_aggregate(dve, 0)
                    v.memset(bufs.zero[:, :], 0.0)
                    v.memset(bufs.fill16[:, 0, :], 0.0)
                    v.memset(bufs.fill16[:, 1, :], 1.0)
                    v.memset(zeros, 0.0).then_inc(zeros_set, 1)
                    for par in range(2):
                        v.memset(bufs.V[par][:, :, :, :], 0.0)
                    v.memset(psum[:, CTX_BANK, :], 0.0)
                    v.tensor_copy(bufs.ident16[:, :], w.ident[:, :]).then_inc(set16, 1)
                    dve.wait_ge(set16, 1)
                    for par in range(2):
                        last = v.memset(bufs.V[par][:, :, :, DK:DK + 1], 1.0)
                    last.then_inc(set16, 1)
                    a.dve_normalise(dve, 0, 0)
                    a.dve_layernorm(dve, 0, 0)
                    a.dve_moments(dve, 1, 1)
                    dve.wait_ge(wa_hi, 1)
                    v.tensor_tensor(bufs.wa[:, LO], raw[:, :], bufs.wa[:, HI].bitcast(F32),
                                    ALU.subtract).then_inc(wa_lo, 1)
                    dve.wait_ge(tab_loaded, 32)
                    v.tensor_copy(bufs.mask16[:, :], raw_mask[:, :]).then_inc(set16, 1)
                    a.dve_hT(dve, 0)
                    dve.wait_ge(set16, 3)
                    a.dve_rope(dve, 0, 0)
                    dve.wait_ge(a.s_stats_ready, 2)
                    a.dve_rest(dve, 0)
                    a.dve_aggregate(dve, 1)
                    for n in range(3):
                        dve.wait_ge(i_hi, n + 1)
                        v.tensor_tensor(iw[n][:, LO], raw_i[n][:, :], iw[n][:, HI].bitcast(F32),
                                        ALU.subtract)
                    for g in range(2):
                        a.dve_max(dve, 0, g)
                        a.dve_max_parts(dve, 0, g, g)
                    a.dve_normalise(dve, 1, 1)

                @block.tensor
                def _(pe):
                    a.pe_hT(pe, 0)
                    pe.wait_ge(wa_lo, 1)
                    for i in range(NT):
                        a.pe_qkv(pe, 0, i)
                    a.pe_qkT(pe, 0)
                    pe.wait_ge(ones_loaded, 32)
                    pe.wait_ge(zeros_loaded, 64)
                    pe.wait_ge(set16, 3)
                    a.pe_max(pe, 0, 0, 0, loads)
                    a.pe_mT(pe, 0, 0, 0)
                    a.pe_max(pe, 0, 1, 0, None)
                    a.pe_mT(pe, 0, 1, 1)

            a = attention("b2b_", attention_uses(), 0)

            def pool_body(pool, b, stats):
                a.pool_mask(pool, b, 0)
                a.pool_parts(pool, b)
                a.pool_mask(pool, b, 1)
                if stats:
                    a.pool_factors(pool, b)
                a.pool_mask(pool, b, 2)
                a.pool_mask(pool, b, 3)

            def act_body(act, b, par):
                a.act_hT(act, b)
                a.act_exp(act, b, 0)
                a.act_exp(act, b, 1, [0])
                a.act_qkT(act, b, b * loads + loads)
                a.act_context(act, b, 0)
                for n in range(2):
                    a.act_exp(act, b, 1, [1 + n])
                    a.act_parts(act, b, n)
                a.act_exp(act, b, 1, range(3, UNITS))
                a.act_mT(act, b, 2, b * (NG * 16) + 32, par)
                a.act_context(act, b, 1)
                a.act_exp(act, b, 2)
                a.act_mT(act, b, 3, b * (NG * 16) + 48, par)
                a.act_context(act, b, 2)
                a.act_exp(act, b, 3)
                a.act_mT(act, b, 0, b * (NG * 16) + 64, 1 - par)
                a.act_context(act, b, 3)
                a.act_cT(act, b)
                a.act_wo(act, b)
                a.act_mT(act, b, 1, b * (NG * 16) + 80, 1 - par)

            def dve_body(dve, b, par, stats):
                nxt = 1 - par
                a.dve_hT(dve, b)
                a.dve_layernorm(dve, b, b + 1)
                a.dve_rope(dve, b, nxt)
                if stats:
                    a.dve_moments(dve, b, b + 2)
                    dve.wait_ge(a.s_stats_ready, b + 1)
                a.dve_rest(dve, b)
                if stats:
                    a.dve_aggregate(dve, b)
                a.dve_max(dve, b, 2)
                a.dve_max_parts(dve, b, 2, 0)
                a.dve_max(dve, b, 3, cut_units(3, CUTS, 0, 3))
                a.dve_ctxT(dve, b, 0)
                a.dve_max(dve, b, 3, cut_units(3, CUTS, 3, 4))
                a.dve_max_parts(dve, b, 3, 1)
                a.dve_max(dve, b, 0, cut_units(0, CUTS, 0, 3))
                a.dve_ctxT(dve, b, 1)
                a.dve_max(dve, b, 0, cut_units(0, CUTS, 3, 4))
                a.dve_max_parts(dve, b, 0, 2)
                a.dve_max(dve, b, 1, cut_units(1, TAIL, 0, 3))
                a.dve_ctxT(dve, b, 2)
                a.dve_max(dve, b, 1, cut_units(1, TAIL, 3, 4))
                a.dve_ctxT(dve, b, 3)
                a.dve_max(dve, b, 1, cut_units(1, TAIL, 4, 5))
                a.dve_cT(dve, b)
                a.dve_max(dve, b, 1, cut_units(1, TAIL, 5, 6))
                a.dve_max_parts(dve, b, 1, 3)
                if stats:
                    a.dve_normalise(dve, b, b + 2)
                a.dve_attn(dve, b, b)

            def beside(pe, a, b, g, par, max_group, max_par, units, first=0):
                left = len(units)
                for u in range(first, UNITS):
                    part = -(-left // (UNITS - u))
                    a.pe_scores(pe, b, g, par, [u])
                    if part:
                        a.pe_max(pe, b, max_group, max_par, None, units[len(units) - left:len(units) - left + part])
                    left -= part

            def context(pe, a, b, g, par, max_group, max_par, units):
                for j in range(NT):
                    a.pe_context(pe, b, g, par, j)
                    a.pe_max(pe, b, max_group, max_par, None, units[j:j + 1])

            def pe_body(pe, b, par):
                nxt = 1 - par
                a.pe_hT(pe, b)
                a.pe_scores(pe, b, 0, par, range(0, 2))
                for i in range(NT):
                    a.pe_qkv(pe, b, i)
                    a.pe_scores(pe, b, 0, par, range(2 + i, min(3 + i, UNITS)))
                a.pe_scores(pe, b, 1, par, [0])
                a.pe_qkT(pe, b)
                context(pe, a, b, 0, par, 2, par, max_units(2)[:BESIDE_0])
                beside(pe, a, b, 1, par, 2, par, max_units(2)[BESIDE_0:], 1)
                a.pe_max(pe, b, 3, par, None, cut_units(3, CUTS, 0, 1))
                a.pe_mT(pe, b, 2, 0)
                a.pe_max(pe, b, 3, par, None, cut_units(3, CUTS, 1, 2))
                context(pe, a, b, 1, par, 3, par, cut_units(3, CUTS, 2, 3))
                a.pe_ctxT(pe, b, 0)
                beside(pe, a, b, 2, par, 3, par, cut_units(3, CUTS, 3, 4))
                a.pe_max(pe, b, 0, nxt, b * loads + 2 * loads, cut_units(0, CUTS, 0, 1))
                a.pe_mT(pe, b, 3, 1)
                a.pe_max(pe, b, 0, nxt, None, cut_units(0, CUTS, 1, 2))
                context(pe, a, b, 2, par, 0, nxt, cut_units(0, CUTS, 2, 3))
                a.pe_ctxT(pe, b, 1)
                beside(pe, a, b, 3, par, 0, nxt, cut_units(0, CUTS, 3, 4))
                a.pe_max(pe, b, 1, nxt, None, cut_units(1, TAIL, 0, 1))
                a.pe_mT(pe, b, 0, 2)
                a.pe_max(pe, b, 1, nxt, None, cut_units(1, TAIL, 1, 2))
                context(pe, a, b, 3, par, 1, nxt, cut_units(1, TAIL, 2, 3))
                a.pe_ctxT(pe, b, 2)
                a.pe_max(pe, b, 1, nxt, None, cut_units(1, TAIL, 3, 4))
                a.pe_ctxT(pe, b, 3)
                a.pe_max(pe, b, 1, nxt, None, cut_units(1, TAIL, 4, 5))
                a.pe_cT(pe, b)
                a.pe_max(pe, b, 1, nxt, None, cut_units(1, TAIL, 5, 6))
                a.pe_wo(pe, b)
                a.pe_mT(pe, b, 1, 3)
                a.pe_attn(pe, b)

            def all_sequences(eng, body):
                with eng.Fori(0, (B - 1) // 2) as pair:
                    for par in range(2):
                        body(pair * 2 + par, par, True)
                body(B - 2, (B - 2) % 2, False)

            with nc.Block() as block:
                @block.sync
                def _(sp):
                    all_sequences(sp, lambda b, par, _: a.load_ext(sp, b, 1 - par, [0, 1]))
                    sp.wait_ge(shared[1], (B - 1) * NG * 16 + 32)

                @block.gpsimd
                def _(pool):
                    pool.sem_inc(a.s_masks, 1)
                    all_sequences(pool, lambda b, par, stats: pool_body(pool, b, stats))

                @block.scalar
                def _(act):
                    act.sem_inc(a.s_act_read, a.plan.per["act"])
                    act.sem_inc(a.s_exps, 2)
                    act.sem_inc(a.s_ctx_read, 1)
                    all_sequences(act, lambda b, par, _: act_body(act, b, par))

                @block.vector
                def _(dve):
                    dve.sem_inc(a.s_dve_read, a.plan.per["dve"])
                    dve.sem_inc(a.s_hn_ready, 1)
                    all_sequences(dve, lambda b, par, stats: dve_body(dve, b, par, stats))

                @block.tensor
                def _(pe):
                    pe.sem_inc(a.s_ctx, NG)
                    all_sequences(pe, lambda b, par, _: pe_body(pe, b, par))

            z = attention("b2c_", last_uses(), B - 1)
            par = (B - 1) % 2
            with nc.Block() as block:
                @block.sync
                def _(sp):
                    sp.wait_ge(shared[1], B * NG * 16)

                @block.gpsimd
                def _(pool):
                    pool.sem_inc(z.s_masks, 1)
                    for g in range(NG):
                        z.pool_mask(pool, 0, g)

                @block.scalar
                def _(act):
                    act.sem_inc(z.s_act_read, z.plan.per["act"])
                    act.sem_inc(z.s_exps, 2)
                    act.sem_inc(z.s_ctx_read, 1)
                    z.act_exp(act, 0, 0)
                    z.act_mT(act, 0, 2, (B - 1) * NG * 16 + 32, par)
                    z.act_exp(act, 0, 1)
                    z.act_mT(act, 0, 3, (B - 1) * NG * 16 + 48, par)
                    z.act_context(act, 0, 0)
                    z.act_exp(act, 0, 2)
                    z.act_context(act, 0, 1)
                    z.act_exp(act, 0, 3)
                    z.act_context(act, 0, 2)
                    z.act_context(act, 0, 3)
                    z.act_cT(act, 0)
                    z.act_wo(act, 0)

                @block.vector
                def _(dve):
                    dve.sem_inc(z.s_dve_read, z.plan.per["dve"])
                    for g in (2, 3):
                        z.dve_max(dve, 0, g)
                        z.dve_max_parts(dve, 0, g, g - 2)
                    for g in range(NG):
                        z.dve_ctxT(dve, 0, g)
                    z.dve_cT(dve, 0)
                    z.dve_attn(dve, 0, B - 1)

                @block.tensor
                def _(pe):
                    pe.sem_inc(z.s_ctx, NG)
                    beside(pe, z, 0, 0, par, 2, par, max_units(2))
                    z.pe_max(pe, 0, 3, par, None, max_units(3)[:4])
                    z.pe_mT(pe, 0, 2, 0)
                    beside(pe, z, 0, 1, par, 3, par, max_units(3)[4:])
                    z.pe_mT(pe, 0, 3, 1)
                    for g in range(NG):
                        context(pe, z, 0, g, par, 3, par, [])
                        if g > 0:
                            z.pe_ctxT(pe, 0, g - 1)
                        if g + 2 < NG:
                            z.pe_scores(pe, 0, g + 2, par)
                    z.pe_ctxT(pe, 0, NG - 1)
                    z.pe_cT(pe, 0)
                    z.pe_wo(pe, 0)
                    z.pe_attn(pe, 0)

        with ExitStack() as scope:
            def sb(name, shape, dt):
                return scope.enter_context(nc.sbuf_tensor("b3_" + name, shape, dt))

            def sem3(name):
                return sem("b3_" + name)

            plan = BankPlan(inner_ffn_uses() + ffn_uses(), FFN_RING)
            fw = FfnWeights(nc, sb, sem3, drams)
            f = Ffn(nc, sb, sem3, psum, w, fw, plan, inner=True)
            stored = sem3("stored")
            w2i = iw[2][:, :, :].rearrange("p n (k o) -> p n k o", k=KC)
            pieces = list(range(5))
            out_pairs = out.rearrange("(n j) (i p) d -> n p j i d", j=2, p=P)
            x_pairs = x[:, :, :, :].rearrange("p (n j) i d -> p n j i d", j=2)

            with nc.Block() as block:
                @block.sync
                def _(sp):
                    fw.sp_load(sp, pieces)
                    with sp.Fori(0, half) as it:
                        sp.wait_ge(f.dve_read, plan.read(it, ("yT", 1)))
                        sp.dma_start(out_pairs[it], x_pairs[:, it]).then_inc(stored, 16)
                    sp.wait_ge(stored, 16 * half)

                @block.gpsimd
                def _(pool):
                    for j in range(2):
                        f.pool_rstd(pool, 0, 0, j, mean_square=True)
                    with pool.Fori(0, half - 1) as it:
                        for j in range(2):
                            f.pool_rstd(pool, it, 1, j, mean_square=False)
                        for j in range(2):
                            f.pool_rstd(pool, it + 1, 0, j, mean_square=True)
                    for j in range(2):
                        f.pool_rstd(pool, half - 1, 1, j, mean_square=False)

                @block.scalar
                def _(act):
                    act.sem_inc(f.act_read, plan.per["act"])

                    def pair(it, following, weights):
                        f.act_first(act, it, 0, "ia", None, 0)
                        fw.act_hi(act, weights[:3])
                        f.act_first(act, it, 1, "ia", None, 0, range(0, 2))
                        f.act_out(act, it, 0, "iy", None)
                        f.act_first(act, it, 1, "ia", None, 0, range(2, KC + 1))
                        f.act_out(act, it, 1, "iy", None)
                        f.act_xT(act, it, 1, 0, None)
                        f.act_outer(act, it, following, w.norms[:, 1:2], weights[3:])

                    for j in range(2):
                        f.act_xT(act, 0, 0, j, w.norms[:, 1:2])
                    pair(0, 1, pieces)
                    with act.Fori(1, half - 1) as it:
                        pair(it, it + 1, [])
                    pair(half - 1, None, [])

                @block.vector
                def _(dve):
                    dve.sem_inc(f.dve_read, plan.per["dve"])
                    dve.sem_inc(f.xT_read, 2)

                    def aggregate(it, which, j):
                        dve.wait_ge(f.stats_ready, f.norm_count(it, which, j))
                        nc.vector.memset(f.spare[:, j:j + 1], 0.0)
                        f.dve_aggregate(dve, j)

                    def flat(v):
                        return v.rearrange("p i d -> p (i d)")

                    def pair(it, following, weights):
                        def first(j, steps):
                            f.dve_first(dve, it, j, "ia", "iu", None, 0, steps)

                        def add(j):
                            f.dve_add(dve, it, j, "iyT", flat(x[:, it * 2 + j]))

                        def moments(j):
                            dve.wait_ge(f.dve_read, plan.read(it, ("iyT", j)))
                            nc.vector.memset(f.spare[:, 2 + j:3 + j], 0.0)
                            f.dve_moments(dve, j, x[:, it * 2 + j])

                        first(0, range(KC + 1))
                        fw.dve_lo(dve, weights[:3])
                        first(1, range(0, 3))
                        add(0)
                        first(1, [3])
                        moments(0)
                        first(1, [4])
                        aggregate(it, 1, 0)
                        f.dve_normalise(dve, it, 1, 0, x[:, it * 2], True)
                        add(1)
                        moments(1)
                        aggregate(it, 1, 1)
                        f.dve_xT(dve, it, 1, 0, None)
                        f.dve_normalise(dve, it, 1, 1, x[:, it * 2 + 1], True)
                        f.dve_first(dve, it, 0, "a", "u", w.scale[:, 1], 0)
                        f.dve_xT(dve, it, 1, 1, None)
                        fw.dve_lo(dve, weights[3:4])
                        f.dve_first(dve, it, 1, "a", "u", w.scale[:, 1], 0)
                        f.dve_outer_rest(dve, it, x, following, y2, w.norms[:, 1:2], False, weights[4:])

                    for j in range(2):
                        f.dve_moments(dve, j, y2[:, j])
                    for j in range(2):
                        aggregate(0, 0, j)
                    for j in range(2):
                        f.dve_normalise(dve, 0, 0, j, y2[:, j], False)
                    for j in range(2):
                        f.dve_xT(dve, 0, 0, j, w.norms[:, 1:2])
                    pair(0, 1, pieces)
                    with dve.Fori(1, half - 1) as it:
                        pair(it, it + 1, [])
                    pair(half - 1, None, [])

                @block.tensor
                def _(pe):
                    def pair(it, following, parts):
                        def first(j, chunks):
                            f.pe_first(pe, it, 0, j, ("ia", "iu"), (iw[0], iw[1]), SPLIT3, chunks)

                        first(0, range(KC))
                        first(1, range(2))
                        f.pe_out(pe, it, 0, "iy", "ia", w2i, 0, SPLIT3)
                        first(1, [2])
                        f.pe_transpose_out(pe, it, 0, "iyT", "iy")
                        first(1, [3])
                        f.pe_out(pe, it, 1, "iy", "ia", w2i, 0, SPLIT3)
                        f.pe_transpose_out(pe, it, 1, "iyT", "iy")
                        f.pe_transpose_in(pe, it, 1, 0)
                        pe.wait_ge(fw.lo_done, 3)
                        f.pe_outer_first(pe, it, 0, parts)
                        f.pe_transpose_in(pe, it, 1, 1)
                        f.pe_outer_first(pe, it, 1, parts)
                        f.pe_outer_rest(pe, it, parts, following)

                    def loop(parts):
                        with pe.Fori(0, half - 1) as it:
                            pair(it, it + 1, parts)
                        pair(half - 1, None, parts)

                    has_lo = pe.value_load(flag[0:1, 0:1])
                    for j in range(2):
                        f.pe_transpose_in(pe, 0, 0, j)
                    with pe.If(has_lo != 0):
                        loop(ALL4)
                    with pe.Else():
                        loop(EXACT_W)


def kernel(**inputs):
    import numpy as np
    import concourse.bacc as bacc
    from concourse.bass_utils import run_bass_kernel_spmd

    a = {k.removeprefix("L0_"): np.asarray(v) for k, v in inputs.items()}
    pos = np.arange(S, dtype=np.float32)
    k = (np.arange(DK) // 2).astype(np.float32)
    angles = pos[:, None] / np.power(np.float32(10000.0), np.float32(2.0) * k / np.float32(DK))
    sign = np.where(np.arange(DK) % 2 == 0, 1.0, -1.0).astype(np.float32)
    cos, sin = np.cos(angles), np.sin(angles) * sign

    def tiles(t):
        return t.reshape(NT, P, DK).transpose(1, 0, 2).reshape(P, NT * DK)

    mask = np.where(np.arange(P)[None, :] > np.arange(P)[:, None], MASKED, 0.0)
    tables = np.concatenate([np.eye(P), mask, tiles(cos), tiles(sin)], axis=1).astype(np.float32)
    arrays = {
        "x": a["attn_x"],
        "ffn_w12": np.stack([a["ffn_w1_w"].T, a["ffn_w2_w"].T]),
        "ffn_h": np.stack([a["ffn_h1_w"].T, a["ffn_h2_w"].T]),
        "ffn_w3": a["ffn_w3_w"].T,
        "ffn_scales": np.stack([a[f"ffn_{n}_s"].reshape(KC, P).T for n in ("w1", "w2", "h1", "h2")], axis=1),
        "ffn_s3": a["ffn_w3_s"].reshape(P, 1),
        "attn_qkvo": np.concatenate([a[f"attn_{n}"].T for n in ("wq", "wk", "wv", "wo")], axis=1),
        "attn_w13": np.stack([a["attn_w1"].T, a["attn_w3"].T]),
        "attn_w2": a["attn_w2"].T,
        "attn_norms": np.stack([a["attn_norm1_w"], a["attn_norm2_w"]], axis=1),
        "tables": tables,
    }
    nc = bacc.Bacc("TRN2", target_bir_lowering=False, num_devices=1)
    fed, args = {}, []
    for name, v in arrays.items():
        v = np.ascontiguousarray(v)
        fed[f"in_{name}"] = v
        args.append(nc.dram_tensor(f"in_{name}", v.shape, mybir.dt.from_np(v.dtype), kind="ExternalInput").ap())
    out = nc.dram_tensor("out_x", (B, S, D), F32, kind="ExternalOutput").ap()
    bass_macaron(nc, *args, out)
    r = run_bass_kernel_spmd(nc, [fed], core_ids=[0])
    return r.results[0]["out_x"]
```
